# Optimizing a Trainium2 kernel written in Bass

```python
import numpy as np
import jax
import jax.numpy as jnp

def _softmax(x, axis=-1):
    return jax.nn.softmax(x, axis=axis)

def _gelu(x):
    return jax.nn.gelu(x, approximate=True)

def _silu(x):
    return jax.nn.silu(x)

def _sigmoid(x):
    return jax.nn.sigmoid(x)

def _layernorm(x, axis=-1, eps=1e-05):
    m = jnp.mean(x, axis=axis, keepdims=True)
    v = jnp.var(x, axis=axis, keepdims=True)
    return (x - m) / jnp.sqrt(v + eps)

def _scatter_add(tgt, idx, src, axis=0):
    return tgt.at[idx].add(src)

def _segment_sum(src, seg, n):
    return jax.ops.segment_sum(src, seg, n)
kernel_name = 'mk_vit_tower_cls_d1_tok_img768_r4_2c2c1e'

def setup_inputs(seed: int=0):
    np.random.seed(seed)
    _w = jnp.asarray

    def _rec_inputs():
        import jax
        import jax.numpy as jnp
        _rk = jax.random.key(seed)
        x = -0.00016672 + 0.999947 * jax.random.normal(jax.random.fold_in(_rk, 1), (16, 96, 96, 3), jnp.float32)
        cls_tok = 0.02 * jax.random.normal(jax.random.fold_in(_rk, 5), (1, 1, 192), jnp.float32)
        return (x, cls_tok)
    x, cls_tok = _rec_inputs()

    def _L0_tok_setup():
        import jax, jax.numpy as jnp
        import numpy as np
        P = 16

        def _extract_patches(images, p):
            B, H, W, C = images.shape
            gh, gw = (H // p, W // p)
            x = images.reshape(B, gh, p, gw, p, C)
            x = x.transpose(0, 1, 3, 2, 4, 5)
            return x.reshape(B, gh * gw, p * p * C)
        key = jax.random.key(seed)
        k1, k2, k3 = jax.random.split(key, 3)
        B, H, Wd, C = (64, 96, 96, 3)
        dims = 192
        patch_dim = P * P * C
        num_patches = H // P * (Wd // P)
        images = jax.random.normal(k1, (B, H, Wd, C), dtype=jnp.float32)
        W = jax.random.normal(k2, (patch_dim, dims), dtype=jnp.float32) * patch_dim ** (-0.5)
        b = jnp.zeros((dims,), dtype=jnp.float32)
        emb_table = jax.random.normal(k3, (num_patches + 2, dims), dtype=jnp.float32) * 0.02
        return {'images': images, 'W': W, 'b': b, 'emb_table': emb_table}
    _L0_tok_all = _L0_tok_setup()
    _L0_tok_in = {k: v for k, v in _L0_tok_all.items() if k in ('W', 'b', 'emb_table')}
    del _L0_tok_all

    def _L0_attn_setup():
        import jax, jax.numpy as jnp
        import numpy as np
        from jax import lax
        B_SZ, L, D, N, R = (1, 1024, 192, 16, 48)

        def _soft_clamp(x, lo=0.0001, hi=10.0):
            center = (hi + lo) / 2.0
            half_range = (hi - lo) / 2.0
            return center + half_range * jnp.tanh((x - center) / half_range)
        key = jax.random.key(seed)
        ks = jax.random.split(key, 6)
        x = jax.random.normal(ks[0], (B_SZ, L, D), jnp.float32)
        A_log = jnp.log(jnp.broadcast_to(jnp.arange(1, N + 1, dtype=jnp.float32), (D, N)))
        D_param = jnp.ones((D,), jnp.float32)
        W_bc = jax.random.normal(ks[1], (D, 2 * N), jnp.float32) / np.sqrt(D).astype(np.float32)
        W_dt = jax.random.normal(ks[2], (D, R), jnp.float32) / np.sqrt(D).astype(np.float32)
        W_dtp = jax.random.normal(ks[3], (R, D), jnp.float32) / np.sqrt(R).astype(np.float32)
        dt = jax.random.uniform(ks[4], (D,), jnp.float32, 0.001, 0.1)
        dt = jnp.clip(dt, 0.0001)
        b_dt = dt + jnp.log(-jnp.expm1(-dt))
        rms_scale = jnp.ones((D,), jnp.float32)
        return {'x': x, 'A_log': A_log, 'D_param': D_param, 'W_bc': W_bc, 'W_dt': W_dt, 'W_dtp': W_dtp, 'b_dt': b_dt, 'rms_scale': rms_scale}
    _L0_attn_all = _L0_attn_setup()
    _L0_attn_in = {k: v for k, v in _L0_attn_all.items() if k in ('A_log', 'D_param', 'W_bc', 'W_dt', 'W_dtp', 'b_dt', 'rms_scale')}
    del _L0_attn_all

    def _L0_ffn_setup():
        import jax, jax.numpy as jnp
        import numpy as np
        B, N, DIM, HEADS = (4, 256, 192, 12)
        HIDDEN, E, TOPK = (768, 8, 2)
        EPS = 1e-05

        def _layernorm(x, g, b):
            mu = jnp.mean(x, axis=-1, keepdims=True)
            var = jnp.var(x, axis=-1, keepdims=True)
            return (x - mu) * jax.lax.rsqrt(var + EPS) * g + b
        key = jax.random.key(seed)
        ks = jax.random.split(key, 10)
        s = 0.02
        return {'x': jax.random.normal(ks[0], (B, N, DIM), dtype=jnp.float32), 'ln1_g': jnp.ones((DIM,), jnp.float32), 'ln1_b': jnp.zeros((DIM,), jnp.float32), 'qkv_w': jax.random.normal(ks[1], (3 * DIM, DIM), jnp.float32) * s, 'proj_w': jax.random.normal(ks[2], (DIM, DIM), jnp.float32) * s, 'proj_b': jnp.zeros((DIM,), jnp.float32), 'ln2_g': jnp.ones((DIM,), jnp.float32), 'ln2_b': jnp.zeros((DIM,), jnp.float32), 'gate_w': jax.random.normal(ks[3], (E, DIM), jnp.float32) * s, 'gate_b': jnp.zeros((E,), jnp.float32), 'w1': jax.random.normal(ks[4], (E, HIDDEN, DIM), jnp.float32) * s, 'b1': jnp.zeros((E, HIDDEN), jnp.float32), 'w2': jax.random.normal(ks[5], (E, DIM, HIDDEN), jnp.float32) * s, 'b2': jnp.zeros((E, DIM), jnp.float32)}
    _L0_ffn_all = _L0_ffn_setup()
    _L0_ffn_in = {k: v for k, v in _L0_ffn_all.items() if k in ('ln1_g', 'ln1_b', 'qkv_w', 'proj_w', 'proj_b', 'ln2_g', 'ln2_b', 'gate_w', 'gate_b', 'w1', 'b1', 'w2', 'b2')}
    del _L0_ffn_all
    return {'x': x, 'cls_tok': cls_tok, 'L0_tok_W': _L0_tok_in['W'], 'L0_tok_b': _L0_tok_in['b'], 'L0_tok_emb_table': _L0_tok_in['emb_table'], 'L0_attn_A_log': _L0_attn_in['A_log'], 'L0_attn_D_param': _L0_attn_in['D_param'], 'L0_attn_W_bc': _L0_attn_in['W_bc'], 'L0_attn_W_dt': _L0_attn_in['W_dt'], 'L0_attn_W_dtp': _L0_attn_in['W_dtp'], 'L0_attn_b_dt': _L0_attn_in['b_dt'], 'L0_attn_rms_scale': _L0_attn_in['rms_scale'], 'L0_ffn_ln1_g': _L0_ffn_in['ln1_g'], 'L0_ffn_ln1_b': _L0_ffn_in['ln1_b'], 'L0_ffn_qkv_w': _L0_ffn_in['qkv_w'], 'L0_ffn_proj_w': _L0_ffn_in['proj_w'], 'L0_ffn_proj_b': _L0_ffn_in['proj_b'], 'L0_ffn_ln2_g': _L0_ffn_in['ln2_g'], 'L0_ffn_ln2_b': _L0_ffn_in['ln2_b'], 'L0_ffn_gate_w': _L0_ffn_in['gate_w'], 'L0_ffn_gate_b': _L0_ffn_in['gate_b'], 'L0_ffn_w1': _L0_ffn_in['w1'], 'L0_ffn_b1': _L0_ffn_in['b1'], 'L0_ffn_w2': _L0_ffn_in['w2'], 'L0_ffn_b2': _L0_ffn_in['b2']}

def reference(x, cls_tok, L0_tok_W, L0_tok_b, L0_tok_emb_table, L0_attn_A_log, L0_attn_D_param, L0_attn_W_bc, L0_attn_W_dt, L0_attn_W_dtp, L0_attn_b_dt, L0_attn_rms_scale, L0_ffn_ln1_g, L0_ffn_ln1_b, L0_ffn_qkv_w, L0_ffn_proj_w, L0_ffn_proj_b, L0_ffn_ln2_g, L0_ffn_ln2_b, L0_ffn_gate_w, L0_ffn_gate_b, L0_ffn_w1, L0_ffn_b1, L0_ffn_w2, L0_ffn_b2):
    import jax
    import jax.numpy as jnp

    def _L0_tok_ref(images, W, b, emb_table):
        import jax, jax.numpy as jnp
        import numpy as np
        P = 16

        def _extract_patches(images, p):
            B, H, W, C = images.shape
            gh, gw = (H // p, W // p)
            x = images.reshape(B, gh, p, gw, p, C)
            x = x.transpose(0, 1, 3, 2, 4, 5)
            return x.reshape(B, gh * gw, p * p * C)
        patches = _extract_patches(images, P)
        x = jnp.einsum('bnd,de->bne', patches, W) + b
        cls = jnp.zeros_like(x[:, :1, :])
        x = jnp.concatenate([cls, x], axis=1)
        n_tok = x.shape[1]
        pos = emb_table[:n_tok]
        return x + pos[None]

    def _L0_attn_ref(x, A_log, D_param, W_bc, W_dt, W_dtp, b_dt, rms_scale):
        import jax, jax.numpy as jnp
        import numpy as np
        from jax import lax
        B_SZ, L, D, N, R = (1, 1024, 192, 16, 48)

        def _soft_clamp(x, lo=0.0001, hi=10.0):
            center = (hi + lo) / 2.0
            half_range = (hi - lo) / 2.0
            return center + half_range * jnp.tanh((x - center) / half_range)
        n = A_log.shape[1]
        A = -jnp.exp(A_log)
        bc = x @ W_bc
        B_sel, C_sel = (bc[..., :n], bc[..., n:])
        delta = jax.nn.softplus(x @ W_dt @ W_dtp + b_dt)
        delta = delta * lax.rsqrt(jnp.mean(delta * delta, axis=-1, keepdims=True) + 1e-06) * rms_scale
        delta = _soft_clamp(delta, 0.0001, 10.0)
        dE = delta[..., None]
        half = 0.5 * dE * A
        denom = 1.0 - half
        A_bar = (1.0 + half) / denom
        B_bar = jnp.sqrt(dE) * B_sel[:, :, None, :] / denom
        x_prev = jnp.concatenate([jnp.zeros_like(x[:, :1]), x[:, :-1]], axis=1)
        x_in = 0.5 * (x + x_prev)
        Bx = B_bar * x_in[..., None]

        def op(left, right):
            a_l, b_l = left
            a_r, b_r = right
            return (a_r * a_l, a_r * b_l + b_r)
        _, all_h = lax.associative_scan(op, (A_bar, Bx), axis=1)
        y = jnp.sum(C_sel[:, :, None, :] * all_h, axis=-1)
        return y + D_param * x

    def _L0_ffn_ref(x, ln1_g, ln1_b, qkv_w, proj_w, proj_b, ln2_g, ln2_b, gate_w, gate_b, w1, b1, w2, b2):
        import jax, jax.numpy as jnp
        import numpy as np
        B, N, DIM, HEADS = (4, 256, 192, 12)
        HIDDEN, E, TOPK = (768, 8, 2)
        EPS = 1e-05

        def _layernorm(x, g, b):
            mu = jnp.mean(x, axis=-1, keepdims=True)
            var = jnp.var(x, axis=-1, keepdims=True)
            return (x - mu) * jax.lax.rsqrt(var + EPS) * g + b
        b, n, d = x.shape
        hd = d // HEADS
        scale = hd ** (-0.5)
        h = _layernorm(x, ln1_g, ln1_b)
        qkv = h @ qkv_w.T
        qkv = qkv.reshape(b, n, 3, HEADS, hd).transpose(2, 0, 3, 1, 4)
        q, k, v = (qkv[0], qkv[1], qkv[2])
        attn = jax.nn.softmax(jnp.einsum('bhnd,bhmd->bhnm', q, k) * scale, axis=-1)
        a = jnp.einsum('bhnm,bhmd->bhnd', attn, v)
        a = a.transpose(0, 2, 1, 3).reshape(b, n, d)
        a = a @ proj_w.T + proj_b
        x = x + a
        h2 = _layernorm(x, ln2_g, ln2_b)
        t = h2.reshape(-1, d)
        T = t.shape[0]
        logits = t @ gate_w.T + gate_b
        top_val, top_idx = jax.lax.top_k(logits, TOPK)
        score = jax.nn.softmax(top_val, axis=-1)
        cw = jnp.zeros((T, E), t.dtype).at[jnp.arange(T)[:, None], top_idx].add(score)
        out = jnp.zeros_like(t)
        for e in range(E):
            he = jax.nn.gelu(t @ w1[e].T + b1[e], approximate=False)
            ye = he @ w2[e].T + b2[e]
            out = out + cw[:, e:e + 1] * ye
        return x + out.reshape(b, n, d)
    h = _L0_tok_ref(x, L0_tok_W, L0_tok_b, L0_tok_emb_table)
    h = jnp.concatenate([jnp.broadcast_to(cls_tok, (h.shape[0], 1, h.shape[2])), h], axis=1)
    h = h + _L0_attn_ref(_layernorm(h, axis=-1), L0_attn_A_log, L0_attn_D_param, L0_attn_W_bc, L0_attn_W_dt, L0_attn_W_dtp, L0_attn_b_dt, L0_attn_rms_scale)
    h = h + _L0_ffn_ref(_layernorm(h, axis=-1), L0_ffn_ln1_g, L0_ffn_ln1_b, L0_ffn_qkv_w, L0_ffn_proj_w, L0_ffn_proj_b, L0_ffn_ln2_g, L0_ffn_ln2_b, L0_ffn_gate_w, L0_ffn_gate_b, L0_ffn_w1, L0_ffn_b1, L0_ffn_w2, L0_ffn_b2)
    return h

_drawn_inputs = setup_inputs


def setup_inputs(seed=0):
    import zlib

    import numpy as np

    out = dict(_drawn_inputs(seed))
    spreads = {'L0_tok_b': (0.0, 0.1),
     'L0_attn_D_param': (1.0, 0.2),
     'L0_attn_rms_scale': (1.0, 0.6),
     'L0_ffn_ln1_g': (1.0, 0.6),
     'L0_ffn_ln1_b': (0.0, 0.8),
     'L0_ffn_proj_b': (0.0, 0.546),
     'L0_ffn_ln2_g': (1.0, 0.6),
     'L0_ffn_ln2_b': (0.0, 0.8),
     'L0_ffn_gate_b': (0.0, 0.423),
     'L0_ffn_b1': (0.0, 0.8),
     'L0_ffn_b2': (0.0, 1.09)}
    factors = {'L0_ffn_qkv_w': 8.0, 'L0_ffn_proj_w': 8.0, 'L0_ffn_w1': 3.065, 'L0_ffn_w2': 2.824}
    for name, (base, spread) in spreads.items():
        noise = np.random.default_rng([zlib.crc32(name.encode()), seed]).standard_normal(out[name].shape)
        drawn = base * np.exp(spread * noise) if base else spread * noise
        out[name] = jnp.asarray(drawn.astype(out[name].dtype))
    for name, factor in factors.items():
        out[name] = (out[name] * factor).astype(out[name].dtype)
    return out
```

```python
import concourse.bass as bass
from concourse import mybir
from contextlib import ExitStack
import numpy as np

BATCH, IMG, CH, PATCH = 16, 96, 3, 16
GRID = IMG // PATCH
NPATCH = GRID * GRID
DIM = 192
PDIM = PATCH * PATCH * CH
TOK = NPATCH + 2
T = BATCH * TOK
GROUPS = 2
GB = BATCH // GROUPS
GT = GB * TOK
GP = GB * NPATCH
CK = 2
CW = DIM // CK
KP = PDIM // 128
NST = 16
RANK = 48
CPT = 128 // NST
TILES = DIM // CPT
TPC = CW // CPT
SUB = 32
TPS = SUB // CPT
STACKS = DIM // SUB
PARTS = 3
HEADS, HD = 12, 16
HPC = HEADS // CK
HG = 3
HGN = HEADS // HG
PAIRS = GB // 2
QROWS = 64
EXP, HIDDEN, TOPK = 8, 768, 2
MT = HIDDEN // 128
SLOTS = 5
TT = (0, 128, GT - 128)
NTT = len(TT)
BANK = 512
SCAN_LAG = 3


def build(nc, a, out):
    f32, bf16, u32 = mybir.dt.float32, mybir.dt.bfloat16, mybir.dt.uint32
    ALU, ACT, AX = mybir.AluOpType, mybir.ActivationFunctionType, mybir.AxisListType
    ctx = ExitStack()
    with ctx:
        def sb(name, shape, dt=f32):
            return ctx.enter_context(nc.sbuf_tensor(name, list(shape), dt))

        def per_group(name, shape, dt=f32):
            return [sb(f"{name}{g}", shape, dt) for g in range(GROUPS)]

        sems = {}

        def S(name, g=None):
            key = name if g is None else f"{name}_{g}"
            if key not in sems:
                sems[key] = ctx.enter_context(nc.semaphore(key))
            return sems[key]

        early = sb("early", [128, max(KP * (GROUPS * GP + DIM), CK * HPC * GT + 2 * HGN * 128)])
        patches = early[:, 0:KP * GROUPS * GP].rearrange("p (k t) -> p k t", k=KP)
        w_tok = early[:, KP * GROUPS * GP:KP * (GROUPS * GP + DIM)].rearrange("p (k d) -> p k d", k=KP)
        kM = early[0:CW, 0:CK * HPC * GT].rearrange("p (c h t) -> p c h t", c=CK, h=HPC)
        prT = early[0:HG * TOK, CK * HPC * GT:CK * HPC * GT + 2 * HGN * 128] \
            .rearrange("p (i n) -> p i n", i=2)
        pos = sb("pos", [CW, CK, NPATCH + 1])
        cols = sb("cols", [CW, CK, 11])
        B_TOK, CLS, D_PAR, B_DT, RMS_S, LN1_G, LN1_B, PROJ_B, LN2_G, LN2_B, SPARE = range(11)
        posb = sb("posb", [CW, CK, NPATCH])
        w_bc = sb("w_bc", [CW, CK, 2, 128])
        w_dt = sb("w_dt", [CW, CK, RANK])
        w_dtp = sb("w_dtp", [RANK, DIM])
        a_log = sb("a_log", [128, TILES])
        abias = sb("abias", [128, TILES])
        w_qkv = sb("w_qkv", [CW, CK, 3 * DIM])
        w_proj = sb("w_proj", [CW, CK, DIM])
        w_gate = sb("w_gate", [CW, CK, EXP])
        b_gate = sb("b_gate", [128, EXP])
        w1 = sb("w1", [CW, CK, SLOTS, HIDDEN])
        b1 = sb("b1", [128, EXP * MT])
        w2 = sb("w2", [128, SLOTS, MT, DIM])
        b2 = sb("b2", [EXP, DIM])
        c_mean = sb("c_mean", [CW, CW])
        acc = per_group("acc", [128, NTT, DIM])
        c_rep = acc[0][0:CW].rearrange("p t d -> p (t d)")[:, 0:TPS * 128]
        c_repb = sb("c_repb", [CW, TPS * 128], bf16)
        c_sum = sb("c_sum", [128, CW - CPT + CPT + CW - CPT])
        c_head = sb("c_head", [CW, HPC])
        c_hblk = sb("c_hblk", [HG * TOK, HG * HD])
        c_eye = sb("c_eye", [128, 128])
        c_iota = sb("c_iota", [128, EXP])
        c_bias = sb("c_bias", [128, 4])
        EPS_LN, EPS_RMS, CLAMP, ZERO = range(4)

        hT = per_group("hT", [CW, CK, GT])
        xn = per_group("xn", [CW, CK, GT])
        cen = per_group("cen", [CW, CK, GT])
        sq = per_group("sq", [CW, CK, GT])
        rs = per_group("rs", [CW, GT])
        b_rep = per_group("b_rep", [128, GT])
        c_repl = per_group("c_repl", [128, GT])
        dtr = per_group("dtr", [RANK, GT])
        t_abs = per_group("t_abs", [CW, CK, GT])
        t_max = per_group("t_max", [CW, CK, GT])
        qT = per_group("qT", [CW, CK, GT + QROWS - TOK])
        t_q = [q[:, :, 0:GT] for q in qT]
        t_u = per_group("t_u", [CW, CK, GT])
        t_l = per_group("t_l", [CW, CK, GT])
        delta = per_group("delta", [CW, CK, GT])
        lng = per_group("lng", [CW, CK, GT])
        uin = per_group("uin", [CW, CK, GT])
        act_h = sb("act_h", [128, 2, MT, GT])
        part_v = act_h[0:CW].rearrange("p i m t -> p (i m t)").bitcast(bf16) \
            .rearrange("p (n c q t) -> p n c q t", n=2 * GROUPS, c=CK, q=PARTS)
        part_g = [part_v[:, g] for g in range(GROUPS)]
        part_u = [part_v[:, GROUPS + g] for g in range(GROUPS)]
        stk_g = per_group("stk_g", [PARTS * SUB, STACKS, GT], bf16)
        stk_u = per_group("stk_u", [PARTS * SUB, STACKS, GT], bf16)
        n1rep = [[x[g][:].rearrange("p k t -> p (k t)").bitcast(f32) for x in (stk_g, stk_u)]
                 for g in range(GROUPS)]
        abar = sb("abar", [128, 3, GT])
        bx = sb("bx", [128, 3, GT])
        hst = sb("hst", [128, 3, GT])
        prod = sb("prod", [128, 3, GT])
        zz, n1, h1 = xn, t_abs, t_max
        vblk = sb("vblk", [HG * TOK, GB, HGN, HG * HD])
        mx = sb("mx", [128, PAIRS, HEADS])
        sm = sb("sm", [128, PAIRS, HEADS])
        rsm = sb("rsm", [128, PAIRS, HEADS])
        sc = bx[:].rearrange("p i t -> p (i t)").rearrange("p (i n) -> p i n", i=2)
        pr = hst[:].rearrange("p i t -> p (i t)").rearrange("p (i n) -> p i n", i=2)
        ao = prod[:].rearrange("p i t -> p (i t)")[:, 0:2 * DIM].rearrange("p (i n) -> p i n", i=2)
        aT, x2, rT, tT = lng, t_u, t_l, delta
        lg = sb("lg", [128, NTT, EXP])
        m8 = sb("m8", [128, NTT, EXP])
        i8 = sb("i8", [128, NTT, EXP], u32)
        i8f = sb("i8f", [128, NTT, EXP])
        gs = sb("gs", [128, 4, NTT])
        cwa = sb("cwa", [128, NTT, EXP])
        cwb = sb("cwb", [128, NTT, EXP])
        cw = per_group("cw", [128, NTT, EXP])
        cwT = [q[0:EXP].rearrange("p c t -> p (c t)")[:, 0:NTT * 128].rearrange("p (t n) -> p t n", t=NTT)
               for q in sq]
        FA = [ctx.enter_context(nc.psum_tensor(f"FA{g}", [128, 2, BANK], f32)) for g in range(GROUPS)]
        FB = [ctx.enter_context(nc.psum_tensor(f"FB{g}", [128, 2, BANK], f32)) for g in range(GROUPS)]
        A0, B0 = FA[0], FB[0]
        UP, DN = FA[1], FB[1]

        block = ctx.enter_context(nc.Block())

        def bcast(ap, axis, n):
            ap = ap.unsqueeze(axis)
            shape = list(ap.shape)
            shape[axis] = n
            return ap.broadcast_to(shape)

        LN_ORDER = [(0, 0), (0, 1), (1, 0), (2, 0), (3, 0), (1, 1), (2, 1), (3, 1)]

        def ln_no(kind, g):
            return LN_ORDER.index((kind, g)) + 1

        LN_IN = {0: hT, 1: h1, 2: zz, 3: x2}
        LN_OUT = {0: xn, 1: zz, 2: n1, 3: tT}

        def fb_of(kind, g):
            return FB[g] if kind == 0 else B0

        def fa_of(kind, g):
            return FA[g] if kind == 0 else A0

        STACKED = 16 * 2 * PARTS * CW // SUB

        def expert_at(x):
            return x if x < EXP else 2 * EXP - 1 - x

        def weights_in(x):
            return 32 if x >= EXP and expert_at(x) < EXP - SLOTS else 16

        @block.sync
        def _(sp):
            sp.dma_start(w_tok[:], a["w_tok"]).then_inc(S("emb_in"), 16)
            for g in range(GROUPS):
                sp.dma_start(patches[:, :, GP * g:GP * (g + 1)],
                             a["patches"][:, :, GP * g:GP * (g + 1)]).then_inc(S("patches_in", g), 16)
            for dst, name in ((w_bc, "w_bc"), (w_dt, "w_dt"), (w_dtp, "w_dtp")):
                sp.dma_start(dst[:], a[name]).then_inc(S("scan_w_in"), 16)
            for dst, name in ((w_qkv, "w_qkv"), (w_proj, "w_proj"), (w_gate, "w_gate"), (b_gate, "b_gate"),
                              (b1, "b1"), (b2, "b2")):
                sp.dma_start(dst[:], a[name]).then_inc(S("attn_w_in"), 16)
            def load_expert(e):
                sp.dma_start(w1[:, :, e % SLOTS, :], a["w1"][:, :, e, :]).then_inc(S("w1_in", e), 16)
                sp.dma_start(w2[:, e % SLOTS], a["w2"][:, e]).then_inc(S("w2_in", e), 16)

            for e in range(SLOTS):
                load_expert(e)
            for g in range(GROUPS):
                for ready, src, dst in (("parts_g", part_g, stk_g), ("parts_u", part_u, stk_u)):
                    sp.wait_ge(S(ready, g), PARTS)
                    for k in range(CW // SUB):
                        for p in range(PARTS):
                            sp.dma_start(
                                dst[g][SUB * p:SUB * (p + 1), k:STACKS:CW // SUB, :],
                                src[g][SUB * k:SUB * (k + 1), :, p, :]).then_inc(S("stacked", g), 16)
            for e in range(SLOTS, EXP):
                sp.wait_ge(S("down_mm"), NTT * (e - SLOTS + 1))
                load_expert(e)
            for e in reversed(range(EXP - SLOTS)):
                sp.wait_ge(S("down_mm"), NTT * (2 * EXP - SLOTS - e))
                load_expert(e)
            for g in range(GROUPS):
                sp.wait_ge(S("acc_done", g), EXP * NTT + 1)
                for t, lo in enumerate(TT):
                    skip = 2 * 128 - GT + 128 if t == NTT - 1 else 0
                    sp.dma_start(out[GT * g + lo + skip:GT * g + lo + 128, :],
                                 acc[g][skip:128, t, :]).then_inc(S("stored"), 16)
            sp.wait_ge(S("stored"), 16 * NTT * GROUPS)

        @block.gpsimd
        def _(pool):
            for g in range(GROUPS):
                pool.memset(qT[g][:, :, GT:], 0.0).then_inc(S("q_pad"), 1)
            for dst, name in ((cols, "cols"), (pos, "pos"), (c_mean, "c_mean"), (a_log, "a_log"),
                              (c_bias, "c_bias"), (c_rep, "c_rep"), (c_sum, "c_sum"),
                              (c_head, "c_head"), (c_hblk, "c_hblk"), (c_eye, "c_eye"), (c_iota, "c_iota")):
                pool.dma_start(dst[:], a[name]).then_inc(S("const_in"), 16)

            def scan_product(g, j):
                n = TILES * g + j
                pool.wait_ge(S("scanned"), n + 1)
                if n >= 3:
                    pool.wait_ge(S("summed"), n - 2)
                if j == 0:
                    pool.wait_ge(S("bc_rep", g), 2)
                nc.gpsimd.tensor_tensor(prod[:, n % 3], hst[:, n % 3], c_repl[g][:], ALU.mult) \
                    .then_inc(S("product"), 1)

            for g in range(GROUPS):
                for j in range(TILES):
                    scan_product(g, j)

        NCONST = 11 * 16

        @block.scalar
        def _(act):
            A = nc.scalar.activation

            def ln(kind, g):
                n = ln_no(kind, g)
                act.wait_ge(S("ln_centred"), n)
                A(sq[g][:], cen[g][:], ACT.Square).then_inc(S("ln_squared"), 1)
                act.wait_ge(S("ln_var"), n)
                A(rs[g][:], fb_of(kind, g)[0:CW, 1, 0:GT], ACT.Ln, bias=c_bias[0:CW, EPS_LN:EPS_LN + 1]) \
                    .then_inc(S("ln_log"), 1)
                act.wait_ge(S("ln_log"), n)
                A(rs[g][:], rs[g][:], ACT.Exp, scale=-0.5).then_inc(S("ln_rstd"), 1)

            def front(g):
                ln(0, g)
                act.wait_ge(S("bc_mm", g), 2)
                A(b_rep[g][:], FA[g][:, 0, 0:GT], ACT.Copy, scale=0.25).then_inc(S("bc_rep", g), 1)
                A(c_repl[g][:], FA[g][:, 1, 0:GT], ACT.Copy).then_inc(S("bc_rep", g), 1)
                act.wait_ge(S("dt_mm", g), 1)
                A(dtr[g][:], FB[g][0:RANK, 0, 0:GT], ACT.Copy).then_inc(S("dt_low", g), 1)
                act.wait_ge(S("dtp_mm", g), 2)
                for c in range(CK):
                    A(t_abs[g][:, c], FB[g][0:CW, c, 0:GT], ACT.Abs, bias=cols[:, c, B_DT:B_DT + 1]) \
                        .then_inc(S("sp_abs", g), 1)
                act.wait_ge(S("sp_abs", g), 2)
                A(t_q[g], t_abs[g][:], ACT.Exp, scale=-1.0).then_inc(S("sp_exp", g), 1)
                act.wait_ge(S("sp_plus1", g), 1)
                A(t_l[g][:], t_u[g][:], ACT.Ln).then_inc(S("sp_ln", g), 1)
                act.wait_ge(S("sp_ln", g), 1)
                A(t_abs[g][:], t_l[g][:], ACT.Exp, scale=-1.0).then_inc(S("sp_inv", g), 1)
                act.wait_ge(S("sp_done", g), 1)
                A(sq[g][:], delta[g][:], ACT.Square).then_inc(S("rms_sq", g), 1)
                act.wait_ge(S("rms_mm", g), 1)
                A(rs[g][:], FA[g][0:CW, 0, 0:GT], ACT.Ln, bias=c_bias[0:CW, EPS_RMS:EPS_RMS + 1]) \
                    .then_inc(S("rms_log", g), 1)
                act.wait_ge(S("rms_log", g), 1)
                A(rs[g][:], rs[g][:], ACT.Exp, scale=-0.5).then_inc(S("rms_rstd", g), 1)

            def clamp(g):
                act.wait_ge(S("rms_done", g), 2)
                A(t_u[g][:], t_q[g], ACT.Tanh, scale=1.0 / HALF,
                  bias=c_bias[0:CW, CLAMP:CLAMP + 1]).then_inc(S("clamp_tanh", g), 1)

            def logs(g):
                act.wait_ge(S("clamped", g), 1)
                A(lng[g][:], delta[g][:], ACT.Ln).then_inc(S("ln_g", g), 1)
                act.wait_ge(S("ln_g", g), 1)
                A(t_l[g][:], lng[g][:], ACT.Exp, scale=0.5).then_inc(S("sqrt_g", g), 1)

            def scan_abar(g, j):
                n = TILES * g + j
                act.wait_ge(S("spread"), n + 1)
                if n >= 3:
                    act.wait_ge(S("scanned"), n - 2)
                A(abar[:, n % 3], A0[:, n % 2, 0:GT], ACT.Tanh, scale=-0.5, bias=abias[:, j:j + 1]) \
                    .then_inc(S("abar"), 1)

            def attention(g):
                for c in range(CK):
                    act.wait_ge(S("qk_mm", g), c + 1)
                    A(qT[g][:, c, 0:GT], A0[0:CW, c, 0:GT], ACT.Copy).then_inc(S("q_done", g), 1)
                act.wait_ge(S("qk_mm", g), CK + 2)
                if g >= 1:
                    act.wait_ge(S("scores"), PAIRS * g)
                for h in range(HPC):
                    A(kM[:, 1, h], B0[0:CW, 1, 0:GT], ACT.Copy, scale=c_head[:, h:h + 1]) \
                        .then_inc(S("k_done"), 1)
                for p in range(PAIRS):
                    n = PAIRS * g + p
                    act.wait_ge(S("shifted"), n + 1)
                    if n >= 2:
                        act.wait_ge(S("probs_T"), n - 1)
                        act.wait_ge(S("prob_sum"), n - 1)
                    A(pr[:, n % 2], sc[:, n % 2], ACT.Exp, scale=HD ** -0.5).then_inc(S("probs"), 1)
                    act.wait_ge(S("probs_T"), n + 1)
                    if n >= 2:
                        act.wait_ge(S("pv"), n - 1)
                    A(prT[:, n % 2], A0[0:HG * TOK, 0, :], ACT.Copy).then_inc(S("probsT_done"), 1)
                    act.wait_ge(S("out_T"), n + 1)
                    for c in range(CK):
                        A(aT[g][:, c, 2 * p * TOK:2 * (p + 1) * TOK].rearrange("p (b t) -> p b t", b=2),
                          B0[0:CW, n % 2, 128 * c:128 * c + 128].rearrange("p (b t) -> p b t", b=2)[:, :, 0:TOK],
                          ACT.Copy).then_inc(S("attn_out"), 1)

            def gate(g):
                act.wait_ge(S("gate_diff", g), 1)
                A(gs[:, 1, :], gs[:, 0, :], ACT.Exp).then_inc(S("gate_exp", g), 1)

            def gelu(x, m):
                n = x * MT + m
                e = expert_at(x)
                if n == 0:
                    act.wait_ge(S("stacked", 1), STACKED)
                act.wait_ge(S("up_mm"), n + 1)
                if x >= 2 and m == 0:
                    act.wait_ge(S("down_mm"), NTT * (x - 1))
                A(act_h[:, x % 2, m], UP[:, n % 2, 0:GT], ACT.Gelu, bias=b1[:, MT * e + m:MT * e + m + 1]) \
                    .then_inc(S("hidden"), 1)

            act.wait_ge(S("const_in"), NCONST)
            for g in range(GROUPS):
                front(g)
            for g in range(GROUPS):
                clamp(g)
            for g in range(GROUPS):
                logs(g)
            act.wait_ge(S("abias"), 1)
            for j in range(TILES):
                scan_abar(0, j)
            for k in (1, 2):
                ln(k, 0)
            attention(0)
            ln(3, 0)
            gate(0)
            act.wait_ge(S("attn_w_in"), 96)
            for step in range(TILES):
                for s in (2 * step, 2 * step + 1):
                    gelu(s // MT, s % MT)
                scan_abar(1, step)
            for k in (1, 2):
                ln(k, 1)
            attention(1)
            ln(3, 1)
            gate(1)
            for s in range(EXP * MT):
                gelu(EXP + s // MT, s % MT)

        @block.vector
        def _(dve):
            V = nc.vector
            TTE, STT, TS = V.tensor_tensor, V.scalar_tensor_tensor, V.tensor_scalar
            count = [0]

            def chain(ins):
                count[0] += 1
                ins.then_inc(S("dve_chain"), 1)
                dve.wait_ge(S("dve_chain"), count[0])

            def ln(kind, g, scale=None, shift=None):
                n = ln_no(kind, g)
                x, y, fb = LN_IN[kind][g], LN_OUT[kind][g], fb_of(kind, g)
                dve.wait_ge(S("ln_mean"), n)
                TTE(cen[g][:], x[:], bcast(fb[0:CW, 0, 0:GT], 1, CK), ALU.subtract).then_inc(S("ln_centred"), 1)
                dve.wait_ge(S("ln_rstd"), n)
                last = TTE(y[:], cen[g][:], bcast(rs[g][:], 1, CK), ALU.mult)
                if scale is not None:
                    chain(last)
                    for c in range(CK):
                        last = TS(y[:, c], y[:, c], cols[:, c, scale:scale + 1], cols[:, c, shift:shift + 1],
                                  ALU.mult, ALU.add)
                        if c < CK - 1:
                            last.then_inc(S("dve_half"), 1)
                last.then_inc(S("ln_out"), 1)

            def front(g):
                dve.wait_ge(S("emb_mm", g), 2)
                hv = hT[g][:].rearrange("p c (b t) -> p c b t", t=TOK)
                pe_v = FA[g][0:CW, :, 0:GP].rearrange("p c (b t) -> p c b t", t=NPATCH)
                V.tensor_copy(hv[:, :, :, 0], bcast(cols[:, :, CLS], 2, GB)).then_inc(S("slots", g), 1)
                V.tensor_copy(hv[:, :, :, 1], bcast(pos[:, :, 0], 2, GB)).then_inc(S("slots", g), 1)
                TTE(hv[:, :, :, 2:], pe_v, bcast(posb[:], 2, GB), ALU.add).then_inc(S("slots", g), 1)
                dve.wait_ge(S("slots", g), 3)
                ln(0, g)
                dve.wait_ge(S("sp_abs", g), 2)
                for c in range(CK):
                    s = FB[g][0:CW, c, 0:GT]
                    bias = cols[:, c, B_DT:B_DT + 1]
                    TS(t_max[g][:, c], s, bias, 0.0, ALU.add, ALU.max).then_inc(S("sp_max", g), 1)
                dve.wait_ge(S("sp_exp", g), 1)
                TS(t_u[g][:], t_q[g], 1.0, None, ALU.add).then_inc(S("sp_plus1", g), 1)
                dve.wait_ge(S("sp_plus1", g), 1)
                STT(out=t_q[g], in0=t_u[g][:], scalar=1.0, in1=t_q[g], op0=ALU.subtract,
                    op1=ALU.subtract).then_inc(S("sp_low", g), 1)
                dve.wait_ge(S("sp_max", g), 2)
                dve.wait_ge(S("sp_ln", g), 1)
                chain(TTE(t_max[g][:], t_max[g][:], t_l[g][:], ALU.add))
                dve.wait_ge(S("sp_inv", g), 1)
                dve.wait_ge(S("sp_low", g), 1)
                chain(TTE(t_q[g], t_q[g], t_abs[g][:], ALU.mult))
                TTE(delta[g][:], t_max[g][:], t_q[g], ALU.subtract).then_inc(S("sp_done", g), 1)
                uv = uin[g][:].rearrange("p c (b t) -> p (c b) t", t=TOK)
                xv = xn[g][:].rearrange("p c (b t) -> p (c b) t", t=TOK)
                TTE(uv[:, :, 1:], xv[:, :, 1:], xv[:, :, :-1], ALU.add).then_inc(S("x_in", g), 1)
                V.tensor_copy(uv[:, :, 0:1], xv[:, :, 0:1]).then_inc(S("x_in", g), 1)
                dve.wait_ge(S("sp_done", g), 1)
                dve.wait_ge(S("rms_rstd", g), 1)
                for c in range(CK):
                    STT(out=t_q[g][:, c], in0=delta[g][:, c], scalar=cols[:, c, RMS_S:RMS_S + 1],
                        in1=rs[g][:], op0=ALU.mult, op1=ALU.mult).then_inc(S("rms_done", g), 1)

            def clamp(g):
                dve.wait_ge(S("clamp_tanh", g), 1)
                TS(delta[g][:], t_u[g][:], HALF, CENTER, ALU.mult, ALU.add).then_inc(S("clamped", g), 1)

            def split(src, parts, g, done):
                V.tensor_copy(parts[:, :, 0], src[:]).then_inc(S(done, g), 1)
                dve.wait_ge(S(done, g), 1)
                chain(TTE(cen[g][:], src[:], parts[:, :, 0], ALU.subtract))
                V.tensor_copy(parts[:, :, 1], cen[g][:]).then_inc(S(done, g), 1)
                dve.wait_ge(S(done, g), 2)
                TTE(parts[:, :, 2], cen[g][:], parts[:, :, 1], ALU.subtract).then_inc(S(done, g), 1)
                dve.wait_ge(S(done, g), 3)

            def splits(g):
                dve.wait_ge(S("ln_g", g), 1)
                split(lng[g], part_g[g], g, "parts_g")
                dve.wait_ge(S("sqrt_g", g), 1)
                dve.wait_ge(S("x_in", g), 2)
                chain(TTE(uin[g][:], uin[g][:], t_l[g][:], ALU.mult))
                split(uin[g], part_u[g], g, "parts_u")

            def scan_input(g, j):
                n = TILES * g + j
                dve.wait_ge(S("spread"), n + 1)
                if j == 0:
                    dve.wait_ge(S("bc_rep", g), 2)
                if n >= 3:
                    dve.wait_ge(S("scanned"), n - 2)
                TTE(bx[:, n % 3], B0[:, 0, 0:GT], b_rep[g][:], ALU.mult).then_inc(S("bx_w"), 1)

            def scan_tile(g, j):
                n = TILES * g + j
                if j + 1 < TILES:
                    scan_input(g, j + 1)
                if j < TILES:
                    dve.wait_ge(S("bx_w"), n + 1)
                    dve.wait_ge(S("abar"), n + 1)
                    STT(out=bx[:, n % 3], in0=abar[:, n % 3], scalar=1.0, in1=bx[:, n % 3],
                        op0=ALU.add, op1=ALU.mult).then_inc(S("bx"), 1)
                if j >= 1:
                    m = n - 1
                    dve.wait_ge(S("reset"), m + 1)
                    dve.wait_ge(S("bx"), m + 1)
                    if m >= 3:
                        dve.wait_ge(S("product"), m - 2)
                    V.tensor_tensor_scan(hst[:, m % 3], abar[:, m % 3], bx[:, m % 3], 0.0,
                                         ALU.mult, ALU.add).then_inc(S("scanned"), 1)
                if j < TILES:
                    dve.wait_ge(S("bx"), n + 1)
                    V.memset(abar[:, n % 3, 0:GT:TOK], 0.0).then_inc(S("reset"), 1)
                if j >= SCAN_LAG + TPC - 1 and (j - SCAN_LAG + 1) % TPC == 0:
                    scan_output(g, (j - SCAN_LAG + 1) // TPC - 1)

            def scan_output(g, c):
                n = TILES * g + TPC * (c + 1)
                dve.wait_ge(S("summed"), n)
                chain(STT(out=h1[g][:, c], in0=xn[g][:, c], scalar=cols[:, c, D_PAR:D_PAR + 1],
                          in1=B0[0:CW, 1, 0:GT], op0=ALU.mult, op1=ALU.add))
                TTE(h1[g][:, c], h1[g][:, c], hT[g][:, c], ALU.add).then_inc(S("scan_out"), 1)

            def attention(g):
                dve.wait_ge(S("ln_out"), ln_no(2, g))
                for c in range(CK):
                    V.tensor_copy(n1rep[g][c].rearrange("p (b r t) -> p b r t", b=GB, r=HG),
                                  bcast(n1[g][:, c].rearrange("p (b t) -> p b t", b=GB), 2, HG)) \
                        .then_inc(S("n1_rep", g), 1)
                for c in range(CK):
                    dve.wait_ge(S("qk_mm", g), CK + c + 1)
                    if c == 0:
                        for h in range(HPC):
                            if g >= 1 and h == 0:
                                dve.wait_ge(S("scores"), PAIRS * g)
                            TS(kM[:, 0, h], B0[0:CW, 0, 0:GT], c_head[:, h:h + 1], None, ALU.mult) \
                                .then_inc(S("k_done"), 1)
                for b in range(GB):
                    n = GB * g + b
                    dve.wait_ge(S("v_mm"), n + 1)
                    if g >= 1 and b == 0:
                        dve.wait_ge(S("pv"), PAIRS * g)
                    TTE(vblk[:, b], A0[0:HG * TOK, b % 2, 0:DIM].rearrange("p (i j) -> p i j", i=HGN),
                        bcast(c_hblk[:], 1, HGN), ALU.mult).then_inc(S("v_done"), 1)

                def shift(p):
                    n = PAIRS * g + p
                    s = B0[:, n % 2, 0:HEADS * TOK].rearrange("p (h k) -> p h k", h=HEADS)
                    dve.wait_ge(S("scores"), n + 1)
                    chain(V.reduce_max(mx[:, p], s, AX.X))
                    if n >= 2:
                        dve.wait_ge(S("probs"), n - 1)
                    TTE(sc[:, n % 2].rearrange("p (h k) -> p h k", h=HEADS), s, bcast(mx[:, p], 2, TOK),
                        ALU.subtract).then_inc(S("shifted"), 1)

                shift(0)
                for p in range(PAIRS):
                    n = PAIRS * g + p
                    if p + 1 < PAIRS:
                        shift(p + 1)
                    dve.wait_ge(S("probs"), n + 1)
                    V.reduce_sum(sm[:, p], pr[:, n % 2].rearrange("p (h k) -> p h k", h=HEADS), AX.X) \
                        .then_inc(S("prob_sum"), 1)
                    dve.wait_ge(S("prob_sum"), n + 1)
                    chain(V.reciprocal(rsm[:, p], sm[:, p]))
                    dve.wait_ge(S("pv"), n + 1)
                    if n >= 2:
                        dve.wait_ge(S("out_T"), n - 1)
                    TTE(ao[:, n % 2].rearrange("p (h d) -> p h d", h=HEADS),
                        A0[:, 1, 0:DIM].rearrange("p (h d) -> p h d", h=HEADS),
                        bcast(rsm[:, p], 2, HD), ALU.mult).then_inc(S("attn_norm"), 1)
                dve.wait_ge(S("proj_mm", g), 2)
                for c in range(CK):
                    STT(out=x2[g][:, c], in0=A0[0:CW, c, 0:GT], scalar=cols[:, c, PROJ_B:PROJ_B + 1],
                        in1=zz[g][:, c], op0=ALU.add, op1=ALU.add).then_inc(S("x2", g), 1)
                dve.wait_ge(S("x2", g), 2)
                TTE(rT[g][:], x2[g][:], h1[g][:], ALU.add).then_inc(S("residual", g), 1)
                ln(3, g, LN2_G, LN2_B)

            def gate(g):
                dve.wait_ge(S("gate_mm", g), 1)
                if g == 0:
                    dve.wait_ge(S("attn_w_in"), 96)
                chain(TTE(lg[:], A0[:, 0, 0:NTT * EXP].rearrange("p (t e) -> p t e", t=NTT),
                          bcast(b_gate[:], 1, NTT), ALU.add))
                for t in range(NTT):
                    last = V.max(m8[:, t], lg[:, t])
                chain(last)
                for t in range(NTT):
                    last = V.max_index(i8[:, t], m8[:, t], lg[:, t])
                chain(last)
                V.tensor_copy(i8f[:], i8[:]).then_inc(S("gate_idx", g), 1)
                TTE(gs[:, 0, :], m8[:, :, 1], m8[:, :, 0], ALU.subtract).then_inc(S("gate_diff", g), 1)
                dve.wait_ge(S("gate_exp", g), 1)
                chain(TS(gs[:, 2, :], gs[:, 1, :], 1.0, None, ALU.add))
                chain(V.reciprocal(gs[:, 2, :], gs[:, 2, :]))
                chain(TTE(gs[:, 3, :], gs[:, 2, :], gs[:, 1, :], ALU.mult))
                dve.wait_ge(S("gate_idx", g), 1)
                for t in range(NTT):
                    TS(cwa[:, t], c_iota[:], i8f[:, t, 0:1], gs[:, 2, t:t + 1], ALU.is_equal, ALU.mult)
                    last = TS(cwb[:, t], c_iota[:], i8f[:, t, 1:2], gs[:, 3, t:t + 1], ALU.is_equal, ALU.mult)
                chain(last)
                TTE(cw[g][:], cwa[:], cwb[:], ALU.add).then_inc(S("cw", g), 1)
                dve.wait_ge(S("cw_T", g), 1)
                V.tensor_copy(cwT[g], A0[0:EXP, 1, 0:NTT * 128].rearrange("p (t n) -> p t n", t=NTT)) \
                    .then_inc(S("cwT_done", g), 1)
                dve.wait_ge(S("acc_mm", g), 2)
                V.tensor_copy(acc[g][:, 0:2], A0[:, 0, 0:2 * DIM].rearrange("p (t d) -> p t d", t=2))
                V.tensor_copy(acc[g][:, 2], A0[:, 1, 0:DIM]).then_inc(S("acc_done", g), 1)

            def accumulate(x, t):
                g, e = x // EXP, expert_at(x)
                n = NTT * x + t
                dve.wait_ge(S("down_mm"), n + 1)
                dve.wait_ge(S("acc_done", g), NTT * (x % EXP - 1) + t + 2 if x % EXP else 1)
                y = DN[:, n % 2, 0:DIM]
                STT(out=acc[g][:, t], in0=y, scalar=cw[g][:, t, e:e + 1], in1=acc[g][:, t],
                    op0=ALU.mult, op1=ALU.add).then_inc(S("acc_done", g), 1)

            dve.wait_ge(S("const_in"), NCONST)
            TS(abias[:], a_log[:], -0.5, 0.5 * float(np.log(2.0)), ALU.mult, ALU.add).then_inc(S("abias"), 1)
            V.tensor_copy(c_repb[:], c_rep[:]).then_inc(S("rep_const"), 1)
            for c in range(CK):
                last = TS(posb[:, c], pos[:, c, 1:], cols[:, c, B_TOK:B_TOK + 1], None, ALU.add)
            chain(last)
            for g in range(GROUPS):
                front(g)
            for g in range(GROUPS):
                clamp(g)
            for g in range(GROUPS):
                splits(g)
            scan_input(0, 0)
            for j in range(TILES + SCAN_LAG):
                if j <= TILES:
                    scan_tile(0, j)
                elif j == TILES + SCAN_LAG - 1:
                    scan_output(0, 1)
            ln(1, 0)
            ln(2, 0, LN1_G, LN1_B)
            attention(0)
            gate(0)
            scan_input(1, 0)
            for j in range(TILES + SCAN_LAG):
                if j <= TILES:
                    scan_tile(1, j)
                elif j == TILES + SCAN_LAG - 1:
                    scan_output(1, 1)
                if 2 <= j < EXP * NTT + 2:
                    accumulate((j - 2) // NTT, (j - 2) % NTT)
            ln(1, 1)
            ln(2, 1, LN1_G, LN1_B)
            attention(1)
            gate(1)
            for e in range(EXP):
                for t in range(NTT):
                    accumulate(EXP + e, t)

        @block.tensor
        def _(pe):
            MM, TR = nc.tensor.matmul, nc.tensor.transpose

            def both(dst, lhs, rhs, lhs_cols):
                for c in range(CK):
                    last = MM(dst, lhs[:, c, lhs_cols], rhs[:, c], start=(c == 0), stop=(c == CK - 1))
                return last

            def ln(kind, g):
                n = ln_no(kind, g)
                x, fb = LN_IN[kind][g], fb_of(kind, g)
                for c in range(CK):
                    last = MM(fb[0:CW, 0, 0:GT], c_mean[:], x[:, c], start=(c == 0), stop=(c == CK - 1))
                last.then_inc(S("ln_mean"), 1)
                pe.wait_ge(S("ln_squared"), n)
                for c in range(CK):
                    last = MM(fb[0:CW, 1, 0:GT], c_mean[:], sq[g][:, c], start=(c == 0), stop=(c == CK - 1))
                last.then_inc(S("ln_var"), 1)

            def embed(g):
                pe.wait_ge(S("patches_in", g), 16)
                for c in range(CK):
                    for k in range(KP):
                        last = MM(FA[g][0:CW, c, 0:GP], w_tok[:, k, CW * c:CW * (c + 1)],
                                  patches[:, k, GP * g:GP * (g + 1)], start=(k == 0), stop=(k == KP - 1))
                    last.then_inc(S("emb_mm", g), 1)

            def front(g):
                pe.wait_ge(S("slots", g), 3)
                ln(0, g)
                pe.wait_ge(S("ln_out"), ln_no(0, g))
                for i in range(2):
                    for c in range(CK):
                        last = MM(FA[g][:, i, 0:GT], w_bc[:, c, i],
                                  xn[g][:, c], start=(c == 0), stop=(c == CK - 1))
                    last.then_inc(S("bc_mm", g), 1)
                for c in range(CK):
                    last = MM(FB[g][0:RANK, 0, 0:GT], w_dt[:, c], xn[g][:, c], start=(c == 0), stop=(c == CK - 1))
                last.then_inc(S("dt_mm", g), 1)
                pe.wait_ge(S("dt_low", g), 1)
                for c in range(CK):
                    MM(FB[g][0:CW, c, 0:GT], w_dtp[:, CW * c:CW * (c + 1)], dtr[g][:], start=True, stop=True) \
                        .then_inc(S("dtp_mm", g), 1)
                pe.wait_ge(S("rms_sq", g), 1)
                pe.wait_ge(S("bc_rep", g), 1)
                for c in range(CK):
                    last = MM(FA[g][0:CW, 0, 0:GT], c_mean[:], sq[g][:, c], start=(c == 0), stop=(c == CK - 1))
                last.then_inc(S("rms_mm", g), 1)

            def spread(g, j):
                n = TILES * g + j
                k = j // TPC * (CW // SUB) + j % TPC // TPS
                if j == 0:
                    pe.wait_ge(S("stacked", g), STACKED)
                    if g >= 1:
                        pe.wait_ge(S("acc_done", g - 1), 1)
                if n >= 2:
                    pe.wait_ge(S("abar"), n - 1)
                sel = c_repb[:, 128 * (j % TPS):128 * (j % TPS + 1)]
                MM(A0[:, n % 2, 0:GT], sel, stk_g[g][:, k], start=True, stop=True)
                if n >= 1:
                    pe.wait_ge(S("bx_w"), n)
                MM(B0[:, 0, 0:GT], sel, stk_u[g][:, k], start=True, stop=True).then_inc(S("spread"), 1)

            def state_sum(g, j):
                n = TILES * g + j
                c, jj = j // TPC, j % TPC
                pe.wait_ge(S("product"), n + 1)
                if jj == 0 and c >= 1:
                    pe.wait_ge(S("scan_out"), CK * g + c)
                lo = CW - CPT - CPT * jj
                MM(B0[0:CW, 1, 0:GT], c_sum[:, lo:lo + CW], prod[:, n % 3], start=(jj == 0),
                   stop=(jj == TPC - 1)).then_inc(S("summed"), 1)

            def scan_step(g, j):
                if j < TILES:
                    spread(g, j)
                if j >= SCAN_LAG:
                    state_sum(g, j - SCAN_LAG)

            def attention(g):
                pe.wait_ge(S("scan_out"), CK * (g + 1))
                ln(1, g)
                pe.wait_ge(S("ln_out"), ln_no(1, g))
                ln(2, g)
                pe.wait_ge(S("ln_out"), ln_no(2, g))
                for bank, base in ((A0, 0), (B0, DIM)):
                    for c in range(CK):
                        both(bank[0:CW, c, 0:GT], w_qkv, n1[g], slice(base + CW * c, base + CW * (c + 1))) \
                            .then_inc(S("qk_mm", g), 1)
                pe.wait_ge(S("n1_rep", g), CK)
                for b in range(GB):
                    n = GB * g + b
                    if b < 2:
                        pe.wait_ge(S("q_done", g), b + 1)
                    else:
                        pe.wait_ge(S("v_done"), n - 1)
                    for c in range(CK):
                        last = MM(A0[0:HG * TOK, b % 2, 0:DIM],
                                  n1rep[g][c][:, HG * TOK * b:HG * TOK * (b + 1)],
                                  w_qkv[:, c, 2 * DIM:3 * DIM], start=(c == 0), stop=(c == CK - 1))
                    last.then_inc(S("v_mm"), 1)

                def scores(p):
                    n = PAIRS * g + p
                    if p == 0:
                        pe.wait_ge(S("q_done", g), 2)
                        pe.wait_ge(S("q_pad"), GROUPS)
                        pe.wait_ge(S("k_done"), HEADS * (g + 1))
                    if p >= 2:
                        pe.wait_ge(S("attn_out"), CK * (n - 1))
                    for half in range(2):
                        lo = TOK * (2 * p + half)
                        for c in range(CK):
                            last = MM(B0[QROWS * half:QROWS * (half + 1), n % 2,
                                         HPC * TOK * c:HPC * TOK * (c + 1)],
                                      qT[g][:, c, lo:lo + QROWS], kM[:, c, :, lo:lo + TOK],
                                      start=True, stop=True)
                    last.then_inc(S("scores"), 1)

                scores(0)
                for p in range(PAIRS):
                    n = PAIRS * g + p
                    if p + 1 < PAIRS:
                        scores(p + 1)
                    pe.wait_ge(S("probs"), n + 1)
                    if p == 0:
                        pe.wait_ge(S("v_done"), GB * (g + 1))
                    else:
                        pe.wait_ge(S("probsT_done"), n)
                    for i in range(HGN):
                        last = TR(A0[0:HG * TOK, 0, 128 * i:128 * (i + 1)],
                                  pr[:, n % 2, HG * TOK * i:HG * TOK * (i + 1)], c_eye[:])
                    last.then_inc(S("probs_T"), 1)
                    pe.wait_ge(S("probsT_done"), n + 1)
                    if p >= 1:
                        pe.wait_ge(S("attn_norm"), n)
                    for half in range(2):
                        for i in range(HGN):
                            last = MM(A0[QROWS * half:QROWS * (half + 1), 1, HG * HD * i:HG * HD * (i + 1)],
                                      prT[:, n % 2, 128 * i + QROWS * half:128 * i + QROWS * (half + 1)],
                                      vblk[:, 2 * p + half, i], start=True, stop=True)
                    last.then_inc(S("pv"), 1)
                    pe.wait_ge(S("attn_norm"), n + 1)
                    for c in range(CK):
                        last = TR(B0[0:CW, n % 2, 128 * c:128 * (c + 1)], ao[:, n % 2, CW * c:CW * (c + 1)],
                                  c_eye[:])
                    last.then_inc(S("out_T"), 1)
                pe.wait_ge(S("attn_out"), CK * PAIRS * (g + 1))
                for c in range(CK):
                    both(A0[0:CW, c, 0:GT], w_proj, aT[g], slice(CW * c, CW * (c + 1))) \
                        .then_inc(S("proj_mm", g), 1)
                pe.wait_ge(S("x2", g), 2)
                ln(3, g)

            def gate(g):
                pe.wait_ge(S("ln_out"), ln_no(3, g))
                for t, lo in enumerate(TT):
                    for c in range(CK):
                        last = MM(A0[:, 0, EXP * t:EXP * (t + 1)], tT[g][:, c, lo:lo + 128], w_gate[:, c],
                                  start=(c == 0), stop=(c == CK - 1))
                last.then_inc(S("gate_mm", g), 1)
                pe.wait_ge(S("cw", g), 1)
                for t in range(NTT):
                    last = TR(A0[0:EXP, 1, 128 * t:128 * (t + 1)], cw[g][:, t], c_eye[:])
                last.then_inc(S("cw_T", g), 1)
                pe.wait_ge(S("cwT_done", g), 1)
                pe.wait_ge(S("residual", g), 1)
                for t, lo in enumerate(TT):
                    dst = A0[:, t // 2, DIM * (t % 2):DIM * (t % 2 + 1)]
                    MM(dst, cwT[g][:, t], b2[:], start=True, stop=False)
                    for c in range(CK):
                        last = MM(dst[:, CW * c:CW * (c + 1)], rT[g][:, c, lo:lo + 128], c_eye[0:CW, 0:CW],
                                  start=False, stop=(c == CK - 1))
                    if t:
                        last.then_inc(S("acc_mm", g), 1)

            def up(x, m):
                n = MT * x + m
                e = expert_at(x)
                if m == 0:
                    pe.wait_ge(S("w1_in", e), weights_in(x))
                if n >= 2:
                    pe.wait_ge(S("hidden"), n - 1)
                both(UP[:, n % 2, 0:GT], w1[:, :, e % SLOTS], tT[x // EXP], slice(128 * m, 128 * (m + 1))) \
                    .then_inc(S("up_mm"), 1)

            def down(x, t):
                e = expert_at(x)
                if t == 0:
                    pe.wait_ge(S("hidden"), MT * (x + 1))
                    pe.wait_ge(S("w2_in", e), weights_in(x))
                n = NTT * x + t
                if n >= 2:
                    y, u = (n - 2) // NTT, (n - 2) % NTT
                    pe.wait_ge(S("acc_done", y // EXP), NTT * (y % EXP) + u + 2)
                for m in range(MT):
                    last = MM(DN[:, n % 2, 0:DIM],
                              act_h[:, x % 2, m, TT[t]:TT[t] + 128], w2[:, e % SLOTS, m],
                              start=(m == 0), stop=(m == MT - 1))
                last.then_inc(S("down_mm"), 1)

            pe.wait_ge(S("emb_in"), 16)
            pe.wait_ge(S("const_in"), NCONST)
            for g in range(GROUPS):
                embed(g)
            pe.wait_ge(S("scan_w_in"), 48)
            for g in range(GROUPS):
                front(g)
            pe.wait_ge(S("rep_const"), 1)
            for j in range(TILES + SCAN_LAG):
                scan_step(0, j)
            pe.wait_ge(S("attn_w_in"), 96)
            attention(0)
            gate(0)
            for e in range(EXP + 1):
                for m in range(MT):
                    if e < EXP:
                        up(e, m)
                    if e >= 1 and m % 2 == 1:
                        down(e - 1, m // 2)
                    if m % 2 == 1:
                        scan_step(1, 3 * e + m // 2)
            attention(1)
            gate(1)
            for e in range(EXP + 1):
                for m in range(MT):
                    if e < EXP:
                        up(EXP + e, m)
                    if e >= 1 and m % 2 == 1:
                        down(EXP + e - 1, m // 2)


LO, HI = 0.0001, 10.0
CENTER, HALF = (HI + LO) / 2.0, (HI - LO) / 2.0
LN_EPS, RMS_EPS = 1e-05, 1e-06


def constants():
    p = np.arange(128)
    rep = np.zeros((PARTS, SUB, TPS, 128), np.float32)
    for j in range(TPS):
        rep[:, CPT * j + p // NST, j, p] = 1.0
    csum = np.zeros((128, 2 * (CW - CPT) + CPT), np.float32)
    csum[p, CW - CPT + p // NST] = 1.0
    head = (np.arange(CW)[:, None] // HD == np.arange(HPC)[None]).astype(np.float32)
    hblk = (np.arange(HG * TOK)[:, None] // TOK == np.arange(HG * HD)[None] // HD).astype(np.float32)
    bias = np.tile(np.array([LN_EPS, RMS_EPS, -CENTER / HALF, 0.0], np.float32), (128, 1))
    return {
        "c_mean": np.full((CW, CW), 1.0 / DIM, np.float32),
        "c_rep": rep.reshape(PARTS * SUB, TPS * 128),
        "c_sum": csum,
        "c_head": head,
        "c_hblk": hblk,
        "c_eye": np.eye(128, dtype=np.float32),
        "c_iota": np.tile(np.arange(EXP, dtype=np.float32), (128, 1)),
        "c_bias": bias,
    }


def layouts(x, cls_tok, L0_tok_W, L0_tok_b, L0_tok_emb_table, L0_attn_A_log, L0_attn_D_param, L0_attn_W_bc,
            L0_attn_W_dt, L0_attn_W_dtp, L0_attn_b_dt, L0_attn_rms_scale, L0_ffn_ln1_g, L0_ffn_ln1_b,
            L0_ffn_qkv_w, L0_ffn_proj_w, L0_ffn_proj_b, L0_ffn_ln2_g, L0_ffn_ln2_b, L0_ffn_gate_w,
            L0_ffn_gate_b, L0_ffn_w1, L0_ffn_b1, L0_ffn_w2, L0_ffn_b2):
    def chunked(w):
        return w.reshape(CK, CW, -1).transpose(1, 0, 2)

    pt = x.reshape(BATCH, GRID, PATCH, GRID, PATCH, CH).transpose(2, 4, 5, 0, 1, 3)
    vecs = np.stack([L0_tok_b, cls_tok.reshape(DIM), L0_attn_D_param, L0_attn_b_dt, L0_attn_rms_scale,
                     L0_ffn_ln1_g, L0_ffn_ln1_b, L0_ffn_proj_b, L0_ffn_ln2_g, L0_ffn_ln2_b,
                     L0_ffn_ln2_b], axis=1)
    return {
        "patches": pt.reshape(KP, 128, BATCH * NPATCH).transpose(1, 0, 2),
        "w_tok": L0_tok_W.reshape(KP, 128, DIM).transpose(1, 0, 2),
        "pos": chunked(L0_tok_emb_table[:NPATCH + 1].T),
        "cols": chunked(vecs),
        "w_bc": np.tile(chunked(L0_attn_W_bc).reshape(CW, CK, 2, 1, NST), (CPT, 1)).reshape(CW, CK, 2, 128),
        "w_dt": chunked(L0_attn_W_dt),
        "w_dtp": L0_attn_W_dtp,
        "a_log": L0_attn_A_log.reshape(TILES, 128).T,
        "w_qkv": chunked(L0_ffn_qkv_w.T),
        "w_proj": chunked(L0_ffn_proj_w.T),
        "w_gate": chunked(L0_ffn_gate_w.T),
        "b_gate": np.broadcast_to(L0_ffn_gate_b, (128, EXP)),
        "w1": L0_ffn_w1.transpose(2, 0, 1).reshape(CK, CW, EXP, HIDDEN).transpose(1, 0, 2, 3),
        "b1": L0_ffn_b1.reshape(EXP * MT, 128).T,
        "w2": L0_ffn_w2.transpose(0, 2, 1).reshape(EXP, MT, 128, DIM).transpose(2, 0, 1, 3),
        "b2": L0_ffn_b2,
    }


def kernel(**inputs):
    import concourse.bacc as bacc
    from concourse.bass_utils import run_bass_kernel_spmd

    nc = bacc.Bacc("TRN2", target_bir_lowering=False, num_devices=1)
    arrays, aps = {}, {}
    data = {**layouts(**{k: np.asarray(v) for k, v in inputs.items()}), **constants()}
    for name, v in data.items():
        v = np.ascontiguousarray(v)
        arrays[f"{name}_dram"] = v
        aps[name] = nc.dram_tensor(f"{name}_dram", v.shape, mybir.dt.from_np(v.dtype), kind="ExternalInput").ap()
    out = nc.dram_tensor("out_dram", (T, DIM), mybir.dt.float32, kind="ExternalOutput").ap()
    build(nc, aps, out)
    r = run_bass_kernel_spmd(nc, [arrays], core_ids=[0])
    return r.results[0]["out_dram"].reshape(BATCH, TOK, DIM)
```

```python
import concourse.bass as bass
from concourse import mybir
from contextlib import ExitStack
import numpy as np

BATCH, IMG, CH, PATCH = 16, 96, 3, 16
GRID = IMG // PATCH
NPATCH = GRID * GRID
DIM = 192
PDIM = PATCH * PATCH * CH
TOK = NPATCH + 2
T = BATCH * TOK
GROUPS = 2
GB = BATCH // GROUPS
GT = GB * TOK
GP = GB * NPATCH
CK = 2
CW = DIM // CK
KP = PDIM // 128
NST = 16
RANK = 48
CPT = 128 // NST
TILES = DIM // CPT
TPC = CW // CPT
SUB = 32
TPS = SUB // CPT
STACKS = DIM // SUB
PARTS = 3
HEADS, HD = 12, 16
HPC = HEADS // CK
HG = 3
HGN = HEADS // HG
PAIRS = GB // 2
QROWS = 64
EXP, HIDDEN, TOPK = 8, 768, 2
MT = HIDDEN // 128
SLOTS = 5
TT = (0, 128, GT - 128)
NTT = len(TT)
BANK = 512
SCAN_LAG = 3


def build(nc, a, out):
    f32, bf16, u32 = mybir.dt.float32, mybir.dt.bfloat16, mybir.dt.uint32
    ALU, ACT, AX = mybir.AluOpType, mybir.ActivationFunctionType, mybir.AxisListType
    ctx = ExitStack()
    with ctx:
        def sb(name, shape, dt=f32):
            return ctx.enter_context(nc.sbuf_tensor(name, list(shape), dt))

        def per_group(name, shape, dt=f32):
            return [sb(f"{name}{g}", shape, dt) for g in range(GROUPS)]

        sems = {}

        def S(name, g=None):
            key = name if g is None else f"{name}_{g}"
            if key not in sems:
                sems[key] = ctx.enter_context(nc.semaphore(key))
            return sems[key]

        early = sb("early", [128, max(KP * (GROUPS * GP + DIM), CK * HPC * GT + 2 * HGN * 128)])
        patches = early[:, 0:KP * GROUPS * GP].rearrange("p (k t) -> p k t", k=KP)
        w_tok = early[:, KP * GROUPS * GP:KP * (GROUPS * GP + DIM)].rearrange("p (k d) -> p k d", k=KP)
        kM = early[0:CW, 0:CK * HPC * GT].rearrange("p (c h t) -> p c h t", c=CK, h=HPC)
        prT = early[0:HG * TOK, CK * HPC * GT:CK * HPC * GT + 2 * HGN * 128] \
            .rearrange("p (i n) -> p i n", i=2)
        pos = sb("pos", [CW, CK, NPATCH + 1])
        cols = sb("cols", [CW, CK, 11])
        B_TOK, CLS, D_PAR, B_DT, RMS_S, LN1_G, LN1_B, PROJ_B, LN2_G, LN2_B, SPARE = range(11)
        posb = sb("posb", [CW, CK, NPATCH])
        w_bc = sb("w_bc", [CW, CK, 2, 128])
        w_dt = sb("w_dt", [CW, CK, RANK])
        w_dtp = sb("w_dtp", [RANK, DIM])
        a_log = sb("a_log", [128, TILES])
        abias = sb("abias", [128, TILES])
        w_qkv = sb("w_qkv", [CW, CK, 3 * DIM])
        w_proj = sb("w_proj", [CW, CK, DIM])
        w_gate = sb("w_gate", [CW, CK, EXP])
        b_gate = sb("b_gate", [128, EXP])
        w1 = sb("w1", [CW, CK, SLOTS, HIDDEN])
        b1 = sb("b1", [128, EXP * MT])
        w2 = sb("w2", [128, SLOTS, MT, DIM])
        b2 = sb("b2", [EXP, DIM])
        c_mean = sb("c_mean", [CW, CW])
        acc = per_group("acc", [128, NTT, DIM])
        c_rep = acc[0][0:CW].rearrange("p t d -> p (t d)")[:, 0:TPS * 128]
        c_repb = sb("c_repb", [CW, TPS * 128], bf16)
        c_sum = sb("c_sum", [128, CW - CPT + CPT + CW - CPT])
        c_head = sb("c_head", [CW, HPC])
        c_hblk = sb("c_hblk", [HG * TOK, HG * HD])
        c_eye = sb("c_eye", [128, 128])
        c_iota = sb("c_iota", [128, EXP])
        c_bias = sb("c_bias", [128, 4])
        EPS_LN, EPS_RMS, CLAMP, ZERO = range(4)

        hT = per_group("hT", [CW, CK, GT])
        xn = per_group("xn", [CW, CK, GT])
        cen = per_group("cen", [CW, CK, GT])
        sq = per_group("sq", [CW, CK, GT])
        rs = per_group("rs", [CW, GT])
        b_rep = per_group("b_rep", [128, GT])
        c_repl = per_group("c_repl", [128, GT])
        dtr = per_group("dtr", [RANK, GT])
        t_abs = per_group("t_abs", [CW, CK, GT])
        t_max = per_group("t_max", [CW, CK, GT])
        qT = per_group("qT", [CW, CK, GT + QROWS - TOK])
        t_q = [q[:, :, 0:GT] for q in qT]
        t_u = per_group("t_u", [CW, CK, GT])
        t_l = per_group("t_l", [CW, CK, GT])
        delta = per_group("delta", [CW, CK, GT])
        lng = per_group("lng", [CW, CK, GT])
        uin = per_group("uin", [CW, CK, GT])
        act_h = sb("act_h", [128, 2, MT, GT])
        part_v = act_h[0:CW].rearrange("p i m t -> p (i m t)").bitcast(bf16) \
            .rearrange("p (n c q t) -> p n c q t", n=2 * GROUPS, c=CK, q=PARTS)
        part_g = [part_v[:, g] for g in range(GROUPS)]
        part_u = [part_v[:, GROUPS + g] for g in range(GROUPS)]
        stk_g = per_group("stk_g", [PARTS * SUB, STACKS, GT], bf16)
        stk_u = per_group("stk_u", [PARTS * SUB, STACKS, GT], bf16)
        n1rep = [[x[g][:].rearrange("p k t -> p (k t)").bitcast(f32) for x in (stk_g, stk_u)]
                 for g in range(GROUPS)]
        scan_buf = sb("scan_buf", [128, 4, 3, GT])
        abar, bx, hst, prod = (scan_buf[:, i] for i in range(4))
        zz, n1, h1 = xn, t_abs, t_max
        vblk = sb("vblk", [HG * TOK, GB, HGN, HG * HD])
        mx = sb("mx", [128, PAIRS, HEADS])
        sm = sb("sm", [128, PAIRS, HEADS])
        rsm = sb("rsm", [128, PAIRS, HEADS])
        pr = scan_buf[:, 0:2].rearrange("p k i t -> p (k i t)").rearrange("p (i n) -> p i n", i=PAIRS)
        ao = [x[:].rearrange("p t d -> p (t d)")[:, 0:2 * DIM].rearrange("p (i n) -> p i n", i=2) for x in acc]
        rs2 = sb("rs2", [CW, GT])
        aT, x2, rT, tT = lng, t_u, t_l, delta
        lg = sb("lg", [128, NTT, EXP])
        m8 = sb("m8", [128, NTT, EXP])
        i8 = sb("i8", [128, NTT, EXP], u32)
        i8f = sb("i8f", [128, NTT, EXP])
        gs = sb("gs", [128, 4, NTT])
        cwa = sb("cwa", [128, NTT, EXP])
        cwb = sb("cwb", [128, NTT, EXP])
        cw = per_group("cw", [128, NTT, EXP])
        cwT = [q[0:EXP].rearrange("p c t -> p (c t)")[:, 0:NTT * 128].rearrange("p (t n) -> p t n", t=NTT)
               for q in sq]
        FA = [ctx.enter_context(nc.psum_tensor(f"FA{g}", [128, 2, BANK], f32)) for g in range(GROUPS)]
        FB = [ctx.enter_context(nc.psum_tensor(f"FB{g}", [128, 2, BANK], f32)) for g in range(GROUPS)]
        A0, B0 = FA[0], FB[0]
        UP, DN = FA[1], FB[1]

        block = ctx.enter_context(nc.Block())

        def bcast(ap, axis, n):
            ap = ap.unsqueeze(axis)
            shape = list(ap.shape)
            shape[axis] = n
            return ap.broadcast_to(shape)

        order = schedule()
        LN_ORDER = [(kind, g) for name, *a_ in order if name == "ln_mean" for kind, g in [a_]]

        def ln_no(kind, g):
            return LN_ORDER.index((kind, g)) + 1

        LN_IN = {0: hT, 1: h1, 3: x2}
        LN_OUT = {0: xn, 1: zz, 3: tT}

        def fb_of(kind, g):
            return FB[g] if kind == 0 else B0

        STACKED = 16 * 2 * PARTS * CW // SUB

        def weights_in(x):
            return 32 if x >= EXP and expert_at(x) < EXP - SLOTS else 16

        def run(steps):
            for name, *args in order:
                if name in steps:
                    steps[name](*args)

        @block.sync
        def _(sp):
            for k in range(0, KP, KP // 2):
                sp.dma_start(w_tok[:, k:k + KP // 2], a["w_tok"][:, k:k + KP // 2]) \
                    .then_inc(S("emb_in", k // (KP // 2)), 16)
                sp.dma_start(patches[:, k:k + KP // 2, 0:GP], a["patches"][:, k:k + KP // 2, 0:GP]) \
                    .then_inc(S("emb_in", k // (KP // 2)), 16)
            sp.dma_start(patches[:, :, GP:], a["patches"][:, :, GP:]).then_inc(S("patches_in", 1), 16)
            for dst, name in ((c_rep, "c_rep"), (c_sum, "c_sum")):
                sp.dma_start(dst[:], a[name]).then_inc(S("scan_const_in"), 16)
            for dst, name in ((w_qkv, "w_qkv"), (w_proj, "w_proj"), (w_gate, "w_gate"), (b_gate, "b_gate"),
                              (b1, "b1"), (b2, "b2"), (c_head, "c_head"), (c_hblk, "c_hblk"), (c_eye, "c_eye"),
                              (c_iota, "c_iota")):
                sp.dma_start(dst[:], a[name]).then_inc(S("attn_w_in"), 16)

            def load_expert(e):
                sp.dma_start(w1[:, :, e % SLOTS, :], a["w1"][:, :, e, :]).then_inc(S("w1_in", e), 16)
                sp.dma_start(w2[:, e % SLOTS], a["w2"][:, e]).then_inc(S("w2_in", e), 16)

            def stack(g):
                for ready, src, dst in (("parts_g", part_g, stk_g), ("parts_u", part_u, stk_u)):
                    sp.wait_ge(S(ready, g), PARTS)
                    for k in range(CW // SUB):
                        for p in range(PARTS):
                            sp.dma_start(
                                dst[g][SUB * p:SUB * (p + 1), k:STACKS:CW // SUB, :],
                                src[g][SUB * k:SUB * (k + 1), :, p, :]).then_inc(S("stacked", g), 16)

            stack(0)
            for e in range(SLOTS):
                load_expert(e)
            stack(1)
            for e in range(SLOTS, EXP):
                sp.wait_ge(S("down_mm"), NTT * (e - SLOTS + 1))
                load_expert(e)
            for e in reversed(range(EXP - SLOTS)):
                sp.wait_ge(S("down_mm"), NTT * (2 * EXP - SLOTS - e))
                load_expert(e)
            for g in range(GROUPS):
                sp.wait_ge(S("acc_done", g), EXP * NTT + 1)
                for t, lo in enumerate(TT):
                    skip = 2 * 128 - GT + 128 if t == NTT - 1 else 0
                    sp.dma_start(out[GT * g + lo + skip:GT * g + lo + 128, :],
                                 acc[g][skip:128, t, :]).then_inc(S("stored"), 16)
            sp.wait_ge(S("stored"), 16 * NTT * GROUPS)

        CONST_IN, SCAN_W_IN, SCAN_CONST_IN, ATTN_W_IN = 16 * 5, 16 * 3, 16 * 2, 16 * 10

        @block.gpsimd
        def _(pool):
            for g in range(GROUPS):
                pool.memset(qT[g][:, :, GT:], 0.0).then_inc(S("q_pad"), 1)

            def scan(g, j):
                if not 2 <= j < TILES + 2:
                    return
                n = TILES * g + j - 2
                pool.wait_ge(S("scanned"), n + 1)
                if n >= 3:
                    pool.wait_ge(S("summed"), n - 2)
                if j == 2:
                    pool.wait_ge(S("bc_rep", g), 2)
                nc.gpsimd.tensor_tensor(prod[:, n % 3], hst[:, n % 3], c_repl[g][:], ALU.mult) \
                    .then_inc(S("product"), 1)

            run({"scan": scan})

        @block.scalar
        def _(act):
            A = nc.scalar.activation
            tables = [None]

            def use(which):
                if tables[0] != which:
                    act.add_instruction(mybir.InstLoadActFuncSet(
                        name=nc.get_next_instruction_name(), engine=mybir.EngineType.Activation,
                        act_func_set_id=which, ins=[], outs=[]))
                    tables[0] = which

            for dst, name in ((cols, "cols"), (pos, "pos"), (c_mean, "c_mean"), (c_bias, "c_bias"),
                              (a_log, "a_log")):
                act.dma_start(dst[:], a[name]).then_inc(S("const_in"), 16)
            for dst, name in ((w_dt, "w_dt"), (w_bc, "w_bc"), (w_dtp, "w_dtp")):
                act.dma_start(dst[:], a[name]).then_inc(S("scan_w_in"), 16)
            use(LN_EXP)
            act.wait_ge(S("const_in"), CONST_IN)

            def ln_mean(kind, g):
                act.wait_ge(S("ln_centred"), ln_no(kind, g))
                A(sq[g][:], cen[g][:], ACT.Square).then_inc(S("ln_squared"), 1)

            def ln_var(kind, g):
                n = ln_no(kind, g)
                use(LN_EXP)
                act.wait_ge(S("ln_var"), n)
                A(rs[g][:], fb_of(kind, g)[0:CW, 1, 0:GT], ACT.Ln, bias=c_bias[0:CW, EPS_LN:EPS_LN + 1]) \
                    .then_inc(S("ln_log"), 1)
                act.wait_ge(S("ln_log"), n)
                A(rs[g][:], rs[g][:], ACT.Exp, scale=-0.5).then_inc(S("ln_rstd"), 1)

            def ln1(g):
                use(LN_EXP)
                act.wait_ge(S("ln1_var", g), 1)
                A(rs2[:], rs2[:], ACT.Ln, bias=c_bias[0:CW, EPS_LN:EPS_LN + 1]).then_inc(S("ln1_log", g), 1)
                act.wait_ge(S("ln1_log", g), 1)
                A(rs2[:], rs2[:], ACT.Exp, scale=-0.5).then_inc(S("ln1_rstd", g), 1)

            def bc(g):
                act.wait_ge(S("dt_mm", g), 1)
                A(dtr[g][:], FB[g][0:RANK, 0, 0:GT], ACT.Copy).then_inc(S("dt_low", g), 1)
                act.wait_ge(S("bc_mm", g), 1)
                A(b_rep[g][:], FA[g][:, 0, 0:GT], ACT.Copy, scale=0.25).then_inc(S("bc_rep", g), 1)
                act.wait_ge(S("bc_mm", g), 2)
                A(c_repl[g][:], FA[g][:, 1, 0:GT], ACT.Copy).then_inc(S("bc_rep", g), 1)

            def dtp(g):
                use(LN_EXP)
                for c in range(CK):
                    act.wait_ge(S("dtp_mm", g), c + 1)
                    A(t_abs[g][:, c], FB[g][0:CW, c, 0:GT], ACT.Abs, bias=cols[:, c, B_DT:B_DT + 1]) \
                        .then_inc(S("sp_abs", g), 1)
                act.wait_ge(S("sp_abs", g), 2)
                A(t_q[g], t_abs[g][:], ACT.Exp, scale=-1.0).then_inc(S("sp_exp", g), 1)

            def softplus(g):
                use(LN_EXP)
                act.wait_ge(S("sp_plus1", g), 1)
                A(t_l[g][:], t_u[g][:], ACT.Ln).then_inc(S("sp_ln", g), 1)
                act.wait_ge(S("sp_ln", g), 1)
                A(t_abs[g][:], t_l[g][:], ACT.Exp, scale=-1.0).then_inc(S("sp_inv", g), 1)

            def rms(g):
                act.wait_ge(S("sp_done", g), 1)
                A(sq[g][:], delta[g][:], ACT.Square).then_inc(S("rms_sq", g), 1)

            def rms_norm(g):
                use(LN_EXP)
                act.wait_ge(S("rms_mm", g), 1)
                A(rs[g][:], FA[g][0:CW, 0, 0:GT], ACT.Ln, bias=c_bias[0:CW, EPS_RMS:EPS_RMS + 1]) \
                    .then_inc(S("rms_log", g), 1)
                act.wait_ge(S("rms_log", g), 1)
                A(rs[g][:], rs[g][:], ACT.Exp, scale=-0.5).then_inc(S("rms_rstd", g), 1)

            def clamp(g):
                use(GELU_TANH)
                act.wait_ge(S("rms_done", g), 2)
                A(t_u[g][:], t_q[g], ACT.Tanh, scale=1.0 / HALF,
                  bias=c_bias[0:CW, CLAMP:CLAMP + 1]).then_inc(S("clamp_tanh", g), 1)

            def logs(g):
                use(LN_EXP)
                act.wait_ge(S("clamped", g), 1)
                A(lng[g][:], delta[g][:], ACT.Ln).then_inc(S("ln_g", g), 1)
                act.wait_ge(S("ln_g", g), 1)
                A(t_l[g][:], lng[g][:], ACT.Exp, scale=0.5).then_inc(S("sqrt_g", g), 1)

            def scan(g, j):
                if j >= TILES:
                    return
                use(GELU_TANH)
                n = TILES * g + j
                if n == 0:
                    act.wait_ge(S("abias"), 1)
                act.wait_ge(S("spread"), n + 1)
                if n >= 3:
                    act.wait_ge(S("scanned"), n - 2)
                if j == 0 and g >= 1:
                    act.wait_ge(S("pv"), PAIRS * g)
                A(abar[:, n % 3], A0[:, n % 2, 0:GT], ACT.Tanh, scale=-0.5, bias=abias[:, j:j + 1]) \
                    .then_inc(S("abar"), 1)

            def qk(g):
                for c in range(CK):
                    act.wait_ge(S("qk_mm", g), c + 1)
                    A(qT[g][:, c, 0:GT], A0[0:CW, c, 0:GT], ACT.Copy).then_inc(S("q_done", g), 1)
                if g == 0:
                    act.wait_ge(S("attn_w_in"), ATTN_W_IN)
                act.wait_ge(S("qk_mm", g), CK + 2)
                if g >= 1:
                    act.wait_ge(S("scores"), PAIRS * g)
                for h in range(HPC):
                    A(kM[:, 1, h], B0[0:CW, 1, 0:GT], ACT.Copy, scale=c_head[:, h:h + 1]) \
                        .then_inc(S("k_done"), 1)

            def exps(g):
                use(LN_EXP)
                for p in range(PAIRS):
                    n = PAIRS * g + p
                    act.wait_ge(S("shifted"), n + 1)
                    A(pr[:, p], pr[:, p], ACT.Exp, scale=HD ** -0.5).then_inc(S("probs"), 1)

            def probs_t(g, p):
                n = PAIRS * g + p
                act.wait_ge(S("probs_T"), n + 1)
                if n >= 2:
                    act.wait_ge(S("pv"), n - 1)
                A(prT[:, n % 2], A0[0:HG * TOK, 0, :], ACT.Copy).then_inc(S("probsT_done"), 1)

            def out_t(g, p):
                n = PAIRS * g + p
                act.wait_ge(S("out_T"), n + 1)
                for c in range(CK):
                    A(aT[g][:, c, 2 * p * TOK:2 * (p + 1) * TOK].rearrange("p (b t) -> p b t", b=2),
                      B0[0:CW, n % 2, 128 * c:128 * c + 128].rearrange("p (b t) -> p b t", b=2)[:, :, 0:TOK],
                      ACT.Copy).then_inc(S("attn_out"), 1)

            def gate_top(g):
                use(GELU_TANH)
                act.wait_ge(S("gate_diff", g), 1)
                A(gs[:, 1, :], gs[:, 0, :], ACT.Tanh, scale=0.5).then_inc(S("gate_tanh", g), 1)

            def up(x, m):
                n = x * MT + m
                use(GELU_TANH)
                if n == 0:
                    act.wait_ge(S("stacked", 1), STACKED)
                    act.wait_ge(S("stacked", 0), STACKED)
                act.wait_ge(S("up_mm"), n + 1)
                if x >= 2 and m == 0:
                    act.wait_ge(S("down_mm"), NTT * (x - 1))
                e = expert_at(x)
                A(act_h[:, x % 2, m], UP[:, n % 2, 0:GT], ACT.Gelu, bias=b1[:, MT * e + m:MT * e + m + 1]) \
                    .then_inc(S("hidden"), 1)

            run({"ln_mean": ln_mean, "ln_var": ln_var, "ln1": ln1, "bc": bc, "dtp": dtp, "softplus": softplus,
                 "rms": rms, "rms_norm": rms_norm, "clamp": clamp, "logs": logs, "scan": scan, "qk": qk,
                 "exps": exps, "probs_t": probs_t, "out_t": out_t, "gate_top": gate_top, "up": up})

        @block.vector
        def _(dve):
            V = nc.vector
            TTE, STT, TS = V.tensor_tensor, V.scalar_tensor_tensor, V.tensor_scalar
            count = [0]

            def chain(ins):
                count[0] += 1
                ins.then_inc(S("dve_chain"), 1)
                dve.wait_ge(S("dve_chain"), count[0])

            dve.wait_ge(S("const_in"), CONST_IN)
            TS(abias[:], a_log[:], -0.5, 0.5 * float(np.log(2.0)), ALU.mult, ALU.add).then_inc(S("abias"), 1)
            for c in range(CK):
                last = TS(posb[:, c], pos[:, c, 1:], cols[:, c, B_TOK:B_TOK + 1], None, ALU.add)
            chain(last)

            def affine(y, scale, shift):
                for c in range(CK):
                    last = TS(y[:, c], y[:, c], cols[:, c, scale:scale + 1], cols[:, c, shift:shift + 1],
                              ALU.mult, ALU.add)
                return last

            def ln_mean(kind, g):
                TTE_in = LN_IN[kind][g]
                dve.wait_ge(S("ln_mean"), ln_no(kind, g))
                TTE(cen[g][:], TTE_in[:], bcast(fb_of(kind, g)[0:CW, 0, 0:GT], 1, CK), ALU.subtract) \
                    .then_inc(S("ln_centred"), 1)

            def ln_var(kind, g):
                y = LN_OUT[kind][g]
                dve.wait_ge(S("ln_rstd"), ln_no(kind, g))
                last = TTE(y[:], cen[g][:], bcast(rs[g][:], 1, CK), ALU.mult)
                if kind == 3:
                    chain(last)
                    last = affine(y, LN2_G, LN2_B)
                last.then_inc(S("ln_out"), 1)
                if kind == 1:
                    chain(TTE(rs2[:], B0[0:CW, 1, 0:GT], rs[g][:], ALU.mult))
                    TTE(rs2[:], rs2[:], rs[g][:], ALU.mult).then_inc(S("ln1_var", g), 1)

            def ln1(g):
                dve.wait_ge(S("ln_out"), ln_no(1, g))
                dve.wait_ge(S("ln1_rstd", g), 1)
                chain(TTE(n1[g][:], zz[g][:], bcast(rs2[:], 1, CK), ALU.mult))
                affine(n1[g], LN1_G, LN1_B).then_inc(S("n1_done", g), 1)

            def embed(g):
                hv = hT[g][:].rearrange("p c (b t) -> p c b t", t=TOK)
                pe_v = FA[g][0:CW, :, 0:GP].rearrange("p c (b t) -> p c b t", t=NPATCH)
                V.tensor_copy(hv[:, :, :, 0], bcast(cols[:, :, CLS], 2, GB)).then_inc(S("slots", g), 1)
                V.tensor_copy(hv[:, :, :, 1], bcast(pos[:, :, 0], 2, GB)).then_inc(S("slots", g), 1)
                dve.wait_ge(S("emb_mm", g), 2)
                TTE(hv[:, :, :, 2:], pe_v, bcast(posb[:], 2, GB), ALU.add).then_inc(S("slots", g), 1)
                dve.wait_ge(S("slots", g), 3)

            def bc(g):
                dve.wait_ge(S("ln_out"), ln_no(0, g))
                uv = uin[g][:].rearrange("p c (b t) -> p (c b) t", t=TOK)
                xv = xn[g][:].rearrange("p c (b t) -> p (c b) t", t=TOK)
                TTE(uv[:, :, 1:], xv[:, :, 1:], xv[:, :, :-1], ALU.add).then_inc(S("x_in", g), 1)
                V.tensor_copy(uv[:, :, 0:1], xv[:, :, 0:1]).then_inc(S("x_in", g), 1)

            def dtp(g):
                for c in range(CK):
                    dve.wait_ge(S("sp_abs", g), c + 1)
                    TS(t_max[g][:, c], FB[g][0:CW, c, 0:GT], cols[:, c, B_DT:B_DT + 1], 0.0, ALU.add, ALU.max) \
                        .then_inc(S("sp_max", g), 1)
                dve.wait_ge(S("sp_exp", g), 1)
                TS(t_u[g][:], t_q[g], 1.0, None, ALU.add).then_inc(S("sp_plus1", g), 1)
                dve.wait_ge(S("sp_plus1", g), 1)
                STT(out=t_q[g], in0=t_u[g][:], scalar=1.0, in1=t_q[g], op0=ALU.subtract,
                    op1=ALU.subtract).then_inc(S("sp_low", g), 1)

            def softplus(g):
                dve.wait_ge(S("sp_max", g), 2)
                dve.wait_ge(S("sp_ln", g), 1)
                chain(TTE(t_max[g][:], t_max[g][:], t_l[g][:], ALU.add))
                dve.wait_ge(S("sp_inv", g), 1)
                dve.wait_ge(S("sp_low", g), 1)
                chain(TTE(t_q[g], t_q[g], t_abs[g][:], ALU.mult))
                TTE(delta[g][:], t_max[g][:], t_q[g], ALU.subtract).then_inc(S("sp_done", g), 1)

            def rms_norm(g):
                dve.wait_ge(S("sp_done", g), 1)
                dve.wait_ge(S("rms_rstd", g), 1)
                for c in range(CK):
                    STT(out=t_q[g][:, c], in0=delta[g][:, c], scalar=cols[:, c, RMS_S:RMS_S + 1],
                        in1=rs[g][:], op0=ALU.mult, op1=ALU.mult).then_inc(S("rms_done", g), 1)

            def clamp(g):
                dve.wait_ge(S("clamp_tanh", g), 1)
                TS(delta[g][:], t_u[g][:], HALF, CENTER, ALU.mult, ALU.add).then_inc(S("clamped", g), 1)

            def split(src, parts, g, done):
                V.tensor_copy(parts[:, :, 0], src[:]).then_inc(S(done, g), 1)
                dve.wait_ge(S(done, g), 1)
                chain(TTE(cen[g][:], src[:], parts[:, :, 0], ALU.subtract))
                V.tensor_copy(parts[:, :, 1], cen[g][:]).then_inc(S(done, g), 1)
                dve.wait_ge(S(done, g), 2)
                TTE(parts[:, :, 2], cen[g][:], parts[:, :, 1], ALU.subtract).then_inc(S(done, g), 1)
                dve.wait_ge(S(done, g), 3)

            def logs(g):
                if g == 0:
                    dve.wait_ge(S("scan_const_in"), SCAN_CONST_IN)
                    V.tensor_copy(c_repb[:], c_rep[:]).then_inc(S("rep_const"), 1)
                dve.wait_ge(S("ln_g", g), 1)
                split(lng[g], part_g[g], g, "parts_g")
                dve.wait_ge(S("sqrt_g", g), 1)
                dve.wait_ge(S("x_in", g), 2)
                chain(TTE(uin[g][:], uin[g][:], t_l[g][:], ALU.mult))
                split(uin[g], part_u[g], g, "parts_u")

            def scan(g, j):
                n = TILES * g + j
                if j == TPC + SCAN_LAG:
                    scan_output(g, 0)
                if j < TILES:
                    dve.wait_ge(S("spread"), n + 1)
                    if j == 0:
                        dve.wait_ge(S("bc_rep", g), 2)
                        if g >= 1:
                            dve.wait_ge(S("pv"), PAIRS * g)
                    if n >= 3:
                        dve.wait_ge(S("scanned"), n - 2)
                    TTE(bx[:, n % 3], B0[:, 0, 0:GT], b_rep[g][:], ALU.mult).then_inc(S("bx_w"), 1)
                if 1 <= j <= TILES:
                    m = n - 1
                    dve.wait_ge(S("bx_w"), m + 1)
                    dve.wait_ge(S("abar"), m + 1)
                    STT(out=bx[:, m % 3], in0=abar[:, m % 3], scalar=1.0, in1=bx[:, m % 3],
                        op0=ALU.add, op1=ALU.mult).then_inc(S("bx"), 1)
                if 2 <= j <= TILES + 1:
                    m = n - 2
                    dve.wait_ge(S("reset"), m + 1)
                    if m >= 3:
                        dve.wait_ge(S("product"), m - 2)
                    V.tensor_tensor_scan(hst[:, m % 3], abar[:, m % 3], bx[:, m % 3], 0.0,
                                         ALU.mult, ALU.add).then_inc(S("scanned"), 1)
                if 1 <= j <= TILES:
                    dve.wait_ge(S("bx"), n)
                    V.memset(abar[:, (n - 1) % 3, 0:GT:TOK], 0.0).then_inc(S("reset"), 1)
                if j == TILES + SCAN_LAG - 1:
                    scan_output(g, 1)

            def scan_output(g, c):
                n = TILES * g + TPC * (c + 1)
                dve.wait_ge(S("summed"), n)
                chain(STT(out=h1[g][:, c], in0=xn[g][:, c], scalar=cols[:, c, D_PAR:D_PAR + 1],
                          in1=B0[0:CW, 1, 0:GT], op0=ALU.mult, op1=ALU.add))
                TTE(h1[g][:, c], h1[g][:, c], hT[g][:, c], ALU.add).then_inc(S("scan_out"), 1)

            def qk(g):
                if g == 0:
                    dve.wait_ge(S("attn_w_in"), ATTN_W_IN)
                dve.wait_ge(S("n1_done", g), 1)
                for c in range(CK):
                    V.tensor_copy(n1rep[g][c].rearrange("p (b r t) -> p b r t", b=GB, r=HG),
                                  bcast(n1[g][:, c].rearrange("p (b t) -> p b t", b=GB), 2, HG)) \
                        .then_inc(S("n1_rep", g), 1)
                dve.wait_ge(S("qk_mm", g), CK + 1)
                if g >= 1:
                    dve.wait_ge(S("scores"), PAIRS * g)
                for h in range(HPC):
                    TS(kM[:, 0, h], B0[0:CW, 0, 0:GT], c_head[:, h:h + 1], None, ALU.mult) \
                        .then_inc(S("k_done"), 1)

            def v(g, b):
                dve.wait_ge(S("v_mm"), GB * g + b + 1)
                if g >= 1 and b == 0:
                    dve.wait_ge(S("pv"), PAIRS * g)
                TTE(vblk[:, b], A0[0:HG * TOK, b % 2, 0:DIM].rearrange("p (i j) -> p i j", i=HGN),
                    bcast(c_hblk[:], 1, HGN), ALU.mult).then_inc(S("v_done"), 1)

            def scores(g, p):
                n = PAIRS * g + p
                s = B0[:, n % 2, 0:HEADS * TOK].rearrange("p (h k) -> p h k", h=HEADS)
                dve.wait_ge(S("scores"), n + 1)
                chain(V.reduce_max(mx[:, p], s, AX.X))
                TTE(pr[:, p].rearrange("p (h k) -> p h k", h=HEADS), s, bcast(mx[:, p], 2, TOK),
                    ALU.subtract).then_inc(S("shifted"), 1)

            def exps(g):
                for p in range(PAIRS):
                    n = PAIRS * g + p
                    dve.wait_ge(S("probs"), n + 1)
                    V.reduce_sum(sm[:, p], pr[:, p].rearrange("p (h k) -> p h k", h=HEADS), AX.X) \
                        .then_inc(S("prob_sum"), 1)
                dve.wait_ge(S("prob_sum"), PAIRS * (g + 1))
                chain(V.reciprocal(rsm[:], sm[:]))

            def pv(g, p):
                n = PAIRS * g + p
                dve.wait_ge(S("pv"), n + 1)
                if p >= 2:
                    dve.wait_ge(S("out_T"), n - 1)
                TTE(ao[g][:, n % 2].rearrange("p (h d) -> p h d", h=HEADS),
                    A0[:, 1, 0:DIM].rearrange("p (h d) -> p h d", h=HEADS),
                    bcast(rsm[:, p], 2, HD), ALU.mult).then_inc(S("attn_norm"), 1)

            def proj(g):
                for c in range(CK):
                    dve.wait_ge(S("proj_mm", g), c + 1)
                    STT(out=x2[g][:, c], in0=A0[0:CW, c, 0:GT], scalar=cols[:, c, PROJ_B:PROJ_B + 1],
                        in1=zz[g][:, c], op0=ALU.add, op1=ALU.add).then_inc(S("x2", g), 1)
                dve.wait_ge(S("x2", g), 2)
                TTE(rT[g][:], x2[g][:], h1[g][:], ALU.add).then_inc(S("residual", g), 1)

            def gate_top(g):
                dve.wait_ge(S("gate_mm", g), 1)
                chain(TTE(lg[:], A0[:, 0, 0:NTT * EXP].rearrange("p (t e) -> p t e", t=NTT),
                          bcast(b_gate[:], 1, NTT), ALU.add))
                for t in range(NTT):
                    last = V.max(m8[:, t], lg[:, t])
                chain(last)
                TTE(gs[:, 0, :], m8[:, :, 1], m8[:, :, 0], ALU.subtract).then_inc(S("gate_diff", g), 1)
                for t in range(NTT):
                    last = V.max_index(i8[:, t], m8[:, t], lg[:, t])
                chain(last)
                V.tensor_copy(i8f[:], i8[:]).then_inc(S("gate_idx", g), 1)

            def gate_weights(g):
                dve.wait_ge(S("gate_tanh", g), 1)
                TS(gs[:, 2, :], gs[:, 1, :], -0.5, 0.5, ALU.mult, ALU.add)
                chain(TS(gs[:, 3, :], gs[:, 1, :], 0.5, 0.5, ALU.mult, ALU.add))
                dve.wait_ge(S("gate_idx", g), 1)
                for t in range(NTT):
                    TS(cwa[:, t], c_iota[:], i8f[:, t, 0:1], gs[:, 2, t:t + 1], ALU.is_equal, ALU.mult)
                    last = TS(cwb[:, t], c_iota[:], i8f[:, t, 1:2], gs[:, 3, t:t + 1], ALU.is_equal, ALU.mult)
                chain(last)
                TTE(cw[g][:], cwa[:], cwb[:], ALU.add).then_inc(S("cw", g), 1)
                dve.wait_ge(S("cw_T", g), 1)
                V.tensor_copy(cwT[g], A0[0:EXP, 1, 0:NTT * 128].rearrange("p (t n) -> p t n", t=NTT)) \
                    .then_inc(S("cwT_done", g), 1)

            def acc_init(g):
                dve.wait_ge(S("acc_mm", g), 2)
                V.tensor_copy(acc[g][:, 0:2], A0[:, 0, 0:2 * DIM].rearrange("p (t d) -> p t d", t=2))
                V.tensor_copy(acc[g][:, 2], A0[:, 1, 0:DIM]).then_inc(S("acc_done", g), 1)

            def down(x, t):
                g, e = x // EXP, expert_at(x)
                n = NTT * x + t
                dve.wait_ge(S("down_mm"), n + 1)
                dve.wait_ge(S("acc_done", g), NTT * (x % EXP - 1) + t + 2 if x % EXP else 1)
                STT(out=acc[g][:, t], in0=DN[:, n % 2, 0:DIM], scalar=cw[g][:, t, e:e + 1],
                    in1=acc[g][:, t], op0=ALU.mult, op1=ALU.add).then_inc(S("acc_done", g), 1)

            run({"embed": embed, "ln_mean": ln_mean, "ln_var": ln_var, "ln1": ln1, "bc": bc, "dtp": dtp,
                 "softplus": softplus, "rms_norm": rms_norm, "clamp": clamp, "logs": logs, "scan": scan,
                 "qk": qk, "v": v, "scores": scores, "exps": exps, "pv": pv, "proj": proj,
                 "gate_top": gate_top, "gate_weights": gate_weights, "acc_init": acc_init, "down": down})

        @block.tensor
        def _(pe):
            MM, TR = nc.tensor.matmul, nc.tensor.transpose

            def both(dst, lhs, rhs, lhs_cols=slice(None)):
                for c in range(CK):
                    last = MM(dst, lhs[:, c, lhs_cols], rhs[:, c], start=(c == 0), stop=(c == CK - 1))
                return last

            def mean_of(dst, x):
                for c in range(CK):
                    last = MM(dst, c_mean[:], x[:, c], start=(c == 0), stop=(c == CK - 1))
                return last

            def embed(g):
                if g:
                    pe.wait_ge(S("patches_in", g), 16)
                for k in range(KP):
                    if g == 0 and k % (KP // 2) == 0:
                        pe.wait_ge(S("emb_in", k // (KP // 2)), 32)
                    for c in range(CK):
                        last = MM(FA[g][0:CW, c, 0:GP], w_tok[:, k, CW * c:CW * (c + 1)],
                                  patches[:, k, GP * g:GP * (g + 1)], start=(k == 0), stop=(k == KP - 1))
                        if k == KP - 1:
                            last.then_inc(S("emb_mm", g), 1)

            def ln_mean(kind, g):
                if kind == 0:
                    pe.wait_ge(S("const_in"), CONST_IN)
                    pe.wait_ge(S("slots", g), 3)
                elif kind == 1:
                    pe.wait_ge(S("scan_out"), CK * (g + 1))
                else:
                    pe.wait_ge(S("x2", g), 2)
                mean_of(fb_of(kind, g)[0:CW, 0, 0:GT], LN_IN[kind][g]).then_inc(S("ln_mean"), 1)

            def ln_var(kind, g):
                pe.wait_ge(S("ln_squared"), ln_no(kind, g))
                mean_of(fb_of(kind, g)[0:CW, 1, 0:GT], sq[g]).then_inc(S("ln_var"), 1)

            def bc(g):
                pe.wait_ge(S("scan_w_in"), SCAN_W_IN)
                pe.wait_ge(S("ln_out"), ln_no(0, g))
                both(FB[g][0:RANK, 0, 0:GT], w_dt, xn[g]).then_inc(S("dt_mm", g), 1)
                for i in range(2):
                    for c in range(CK):
                        last = MM(FA[g][:, i, 0:GT], w_bc[:, c, i], xn[g][:, c],
                                  start=(c == 0), stop=(c == CK - 1))
                    last.then_inc(S("bc_mm", g), 1)

            def dtp(g):
                pe.wait_ge(S("dt_low", g), 1)
                for c in range(CK):
                    MM(FB[g][0:CW, c, 0:GT], w_dtp[:, CW * c:CW * (c + 1)], dtr[g][:], start=True, stop=True) \
                        .then_inc(S("dtp_mm", g), 1)

            def rms(g):
                pe.wait_ge(S("rms_sq", g), 1)
                pe.wait_ge(S("bc_rep", g), 1)
                mean_of(FA[g][0:CW, 0, 0:GT], sq[g]).then_inc(S("rms_mm", g), 1)

            def scan(g, j):
                if j < TILES:
                    spread(g, j)
                if SCAN_LAG <= j:
                    state_sum(g, j - SCAN_LAG)

            def spread(g, j):
                n = TILES * g + j
                k = j // TPC * (CW // SUB) + j % TPC // TPS
                if j == 0:
                    pe.wait_ge(S("stacked", g), STACKED)
                    if g == 0:
                        pe.wait_ge(S("rep_const"), 1)
                        pe.wait_ge(S("scan_const_in"), SCAN_CONST_IN)
                    else:
                        pe.wait_ge(S("acc_done", g - 1), 1)
                if n >= 2:
                    pe.wait_ge(S("abar"), n - 1)
                sel = c_repb[:, 128 * (j % TPS):128 * (j % TPS + 1)]
                MM(A0[:, n % 2, 0:GT], sel, stk_g[g][:, k], start=True, stop=True)
                if n >= 1:
                    pe.wait_ge(S("bx_w"), n)
                MM(B0[:, 0, 0:GT], sel, stk_u[g][:, k], start=True, stop=True).then_inc(S("spread"), 1)

            def state_sum(g, j):
                n = TILES * g + j
                c, jj = j // TPC, j % TPC
                pe.wait_ge(S("product"), n + 1)
                if jj == 0 and c >= 1:
                    pe.wait_ge(S("scan_out"), CK * g + c)
                lo = CW - CPT - CPT * jj
                MM(B0[0:CW, 1, 0:GT], c_sum[:, lo:lo + CW], prod[:, n % 3], start=(jj == 0),
                   stop=(jj == TPC - 1)).then_inc(S("summed"), 1)

            def qk(g):
                if g == 0:
                    pe.wait_ge(S("attn_w_in"), ATTN_W_IN)
                pe.wait_ge(S("n1_done", g), 1)
                for bank, base in ((A0, 0), (B0, DIM)):
                    for c in range(CK):
                        both(bank[0:CW, c, 0:GT], w_qkv, n1[g], slice(base + CW * c, base + CW * (c + 1))) \
                            .then_inc(S("qk_mm", g), 1)

            def v(g, b):
                if b < 2:
                    pe.wait_ge(S("n1_rep", g), CK)
                    pe.wait_ge(S("q_done", g), b + 1)
                else:
                    pe.wait_ge(S("v_done"), GB * g + b - 1)
                for c in range(CK):
                    last = MM(A0[0:HG * TOK, b % 2, 0:DIM], n1rep[g][c][:, HG * TOK * b:HG * TOK * (b + 1)],
                              w_qkv[:, c, 2 * DIM:3 * DIM], start=(c == 0), stop=(c == CK - 1))
                last.then_inc(S("v_mm"), 1)

            def scores(g, p):
                n = PAIRS * g + p
                if p == 0:
                    pe.wait_ge(S("q_done", g), 2)
                    pe.wait_ge(S("q_pad"), GROUPS)
                    pe.wait_ge(S("k_done"), HEADS * (g + 1))
                if p >= 2:
                    pe.wait_ge(S("shifted"), n - 1)
                for half in range(2):
                    lo = TOK * (2 * p + half)
                    for c in range(CK):
                        last = MM(B0[QROWS * half:QROWS * (half + 1), n % 2,
                                     HPC * TOK * c:HPC * TOK * (c + 1)],
                                  qT[g][:, c, lo:lo + QROWS], kM[:, c, :, lo:lo + TOK],
                                  start=True, stop=True)
                last.then_inc(S("scores"), 1)

            def probs_t(g, p):
                n = PAIRS * g + p
                pe.wait_ge(S("probs"), n + 1)
                if p == 0:
                    pe.wait_ge(S("v_done"), GB * (g + 1))
                else:
                    pe.wait_ge(S("probsT_done"), n)
                for i in range(HGN):
                    last = TR(A0[0:HG * TOK, 0, 128 * i:128 * (i + 1)],
                              pr[:, p, HG * TOK * i:HG * TOK * (i + 1)], c_eye[:])
                last.then_inc(S("probs_T"), 1)

            def pv(g, p):
                n = PAIRS * g + p
                pe.wait_ge(S("probsT_done"), n + 1)
                if p >= 1:
                    pe.wait_ge(S("attn_norm"), n)
                for half in range(2):
                    for i in range(HGN):
                        last = MM(A0[QROWS * half:QROWS * (half + 1), 1, HG * HD * i:HG * HD * (i + 1)],
                                  prT[:, n % 2, 128 * i + QROWS * half:128 * i + QROWS * (half + 1)],
                                  vblk[:, 2 * p + half, i], start=True, stop=True)
                last.then_inc(S("pv"), 1)

            def out_t(g, p):
                n = PAIRS * g + p
                pe.wait_ge(S("attn_norm"), n + 1)
                if p == 0:
                    pe.wait_ge(S("shifted"), PAIRS * (g + 1))
                if p >= 2:
                    pe.wait_ge(S("attn_out"), CK * (n - 1))
                for c in range(CK):
                    last = TR(B0[0:CW, n % 2, 128 * c:128 * (c + 1)], ao[g][:, n % 2, CW * c:CW * (c + 1)],
                              c_eye[:])
                last.then_inc(S("out_T"), 1)

            def proj(g):
                pe.wait_ge(S("attn_out"), CK * PAIRS * (g + 1))
                for c in range(CK):
                    both(A0[0:CW, c, 0:GT], w_proj, aT[g], slice(CW * c, CW * (c + 1))) \
                        .then_inc(S("proj_mm", g), 1)

            def gate_top(g):
                pe.wait_ge(S("ln_out"), ln_no(3, g))
                for t, lo in enumerate(TT):
                    for c in range(CK):
                        last = MM(A0[:, 0, EXP * t:EXP * (t + 1)], tT[g][:, c, lo:lo + 128], w_gate[:, c],
                                  start=(c == 0), stop=(c == CK - 1))
                last.then_inc(S("gate_mm", g), 1)

            def gate_weights(g):
                pe.wait_ge(S("cw", g), 1)
                for t in range(NTT):
                    last = TR(A0[0:EXP, 1, 128 * t:128 * (t + 1)], cw[g][:, t], c_eye[:])
                last.then_inc(S("cw_T", g), 1)

            def acc_init(g):
                pe.wait_ge(S("cwT_done", g), 1)
                pe.wait_ge(S("residual", g), 1)
                for t, lo in enumerate(TT):
                    dst = A0[:, t // 2, DIM * (t % 2):DIM * (t % 2 + 1)]
                    MM(dst, cwT[g][:, t], b2[:], start=True, stop=False)
                    for c in range(CK):
                        last = MM(dst[:, CW * c:CW * (c + 1)], rT[g][:, c, lo:lo + 128], c_eye[0:CW, 0:CW],
                                  start=False, stop=(c == CK - 1))
                    if t:
                        last.then_inc(S("acc_mm", g), 1)

            def up(x, m):
                n = MT * x + m
                e = expert_at(x)
                if m == 0:
                    pe.wait_ge(S("w1_in", e), weights_in(x))
                if n >= 2:
                    pe.wait_ge(S("hidden"), n - 1)
                both(UP[:, n % 2, 0:GT], w1[:, :, e % SLOTS], tT[x // EXP], slice(128 * m, 128 * (m + 1))) \
                    .then_inc(S("up_mm"), 1)

            def down(x, t):
                e = expert_at(x)
                if t == 0:
                    pe.wait_ge(S("hidden"), MT * (x + 1))
                    pe.wait_ge(S("w2_in", e), weights_in(x))
                n = NTT * x + t
                if n >= 2:
                    y, u = (n - 2) // NTT, (n - 2) % NTT
                    pe.wait_ge(S("acc_done", y // EXP), NTT * (y % EXP) + u + 2)
                for m in range(MT):
                    last = MM(DN[:, n % 2, 0:DIM], act_h[:, x % 2, m, TT[t]:TT[t] + 128],
                              w2[:, e % SLOTS, m], start=(m == 0), stop=(m == MT - 1))
                last.then_inc(S("down_mm"), 1)

            run({"embed": embed, "ln_mean": ln_mean, "ln_var": ln_var, "bc": bc, "dtp": dtp, "rms": rms,
                 "scan": scan, "qk": qk, "v": v, "scores": scores, "probs_t": probs_t, "pv": pv,
                 "out_t": out_t, "proj": proj, "gate_top": gate_top, "gate_weights": gate_weights,
                 "acc_init": acc_init, "up": up, "down": down})


def expert_at(x):
    return x if x < EXP else 2 * EXP - 1 - x


def schedule():
    def front(g):
        return [(("embed", g), 1), (("ln_mean", 0, g), 2), (("ln_var", 0, g), 3), (("bc", g), 1),
                (("dtp", g), 3), (("softplus", g), 3), (("rms", g), 1), (("rms_norm", g), 2),
                (("clamp", g), 2), (("logs", g), 4)]

    def scan(g):
        return [(("scan", g, j), 1) for j in range(TILES + SCAN_LAG)]

    def attention(g):
        steps = [(("ln_mean", 1, g), 2), (("ln_var", 1, g), 2), (("ln1", g), 3), (("qk", g), 1)]
        steps += [(("v", g, b), 0) for b in range(GB)]
        steps += [(("scores", g, p), 1) for p in range(PAIRS)]
        steps += [(("exps", g), 3)]
        for p in range(PAIRS):
            steps += [(("probs_t", g, p), 1), (("pv", g, p), 1), (("out_t", g, p), 0)]
        return steps + [(("proj", g), 2), (("ln_mean", 3, g), 2), (("ln_var", 3, g), 4),
                        (("gate_top", g), 3), (("gate_weights", g), 1), (("acc_init", g), 1)]

    def experts(g):
        steps = []
        for e in range(EXP + 1):
            for m in range(MT):
                if e < EXP:
                    steps.append((("up", EXP * g + e, m), 1))
                if e >= 1 and m % 2 == 1:
                    steps.append((("down", EXP * g + e - 1, m // 2), 2))
        return steps

    def weave(main, filler):
        order, filler, room = [], list(filler), 0
        for step, free in main:
            order.append(step)
            room += free
            while filler and room > 0:
                order.append(filler[0][0])
                room -= filler.pop(0)[1]
        return order + [step for step, _ in filler]

    order = [step for step, _ in front(0) + scan(0)]
    order += weave(attention(0), front(1))
    order += weave(scan(1) + attention(1), experts(0))
    return order + [step for step, _ in experts(1)]


LO, HI = 0.0001, 10.0
CENTER, HALF = (HI + LO) / 2.0, (HI - LO) / 2.0
LN_EPS, RMS_EPS = 1e-05, 1e-06
LN_EXP, GELU_TANH = 6, 10


def constants():
    p = np.arange(128)
    rep = np.zeros((PARTS, SUB, TPS, 128), np.float32)
    for j in range(TPS):
        rep[:, CPT * j + p // NST, j, p] = 1.0
    csum = np.zeros((128, 2 * (CW - CPT) + CPT), np.float32)
    csum[p, CW - CPT + p // NST] = 1.0
    head = (np.arange(CW)[:, None] // HD == np.arange(HPC)[None]).astype(np.float32)
    hblk = (np.arange(HG * TOK)[:, None] // TOK == np.arange(HG * HD)[None] // HD).astype(np.float32)
    bias = np.tile(np.array([LN_EPS, RMS_EPS, -CENTER / HALF, 0.0], np.float32), (128, 1))
    return {
        "c_mean": np.full((CW, CW), 1.0 / DIM, np.float32),
        "c_rep": rep.reshape(PARTS * SUB, TPS * 128),
        "c_sum": csum,
        "c_head": head,
        "c_hblk": hblk,
        "c_eye": np.eye(128, dtype=np.float32),
        "c_iota": np.tile(np.arange(EXP, dtype=np.float32), (128, 1)),
        "c_bias": bias,
    }


def layouts(x, cls_tok, L0_tok_W, L0_tok_b, L0_tok_emb_table, L0_attn_A_log, L0_attn_D_param, L0_attn_W_bc,
            L0_attn_W_dt, L0_attn_W_dtp, L0_attn_b_dt, L0_attn_rms_scale, L0_ffn_ln1_g, L0_ffn_ln1_b,
            L0_ffn_qkv_w, L0_ffn_proj_w, L0_ffn_proj_b, L0_ffn_ln2_g, L0_ffn_ln2_b, L0_ffn_gate_w,
            L0_ffn_gate_b, L0_ffn_w1, L0_ffn_b1, L0_ffn_w2, L0_ffn_b2):
    def chunked(w):
        return w.reshape(CK, CW, -1).transpose(1, 0, 2)

    pt = x.reshape(BATCH, GRID, PATCH, GRID, PATCH, CH).transpose(2, 4, 5, 0, 1, 3)
    vecs = np.stack([L0_tok_b, cls_tok.reshape(DIM), L0_attn_D_param, L0_attn_b_dt, L0_attn_rms_scale,
                     L0_ffn_ln1_g, L0_ffn_ln1_b, L0_ffn_proj_b, L0_ffn_ln2_g, L0_ffn_ln2_b,
                     L0_ffn_ln2_b], axis=1)
    return {
        "patches": pt.reshape(KP, 128, BATCH * NPATCH).transpose(1, 0, 2),
        "w_tok": L0_tok_W.reshape(KP, 128, DIM).transpose(1, 0, 2),
        "pos": chunked(L0_tok_emb_table[:NPATCH + 1].T),
        "cols": chunked(vecs),
        "w_bc": np.tile(chunked(L0_attn_W_bc).reshape(CW, CK, 2, 1, NST), (CPT, 1)).reshape(CW, CK, 2, 128),
        "w_dt": chunked(L0_attn_W_dt),
        "w_dtp": L0_attn_W_dtp,
        "a_log": L0_attn_A_log.reshape(TILES, 128).T,
        "w_qkv": chunked(L0_ffn_qkv_w.T),
        "w_proj": chunked(L0_ffn_proj_w.T),
        "w_gate": chunked(L0_ffn_gate_w.T),
        "b_gate": np.broadcast_to(L0_ffn_gate_b, (128, EXP)),
        "w1": L0_ffn_w1.transpose(2, 0, 1).reshape(CK, CW, EXP, HIDDEN).transpose(1, 0, 2, 3),
        "b1": L0_ffn_b1.reshape(EXP * MT, 128).T,
        "w2": L0_ffn_w2.transpose(0, 2, 1).reshape(EXP, MT, 128, DIM).transpose(2, 0, 1, 3),
        "b2": L0_ffn_b2,
    }


def kernel(**inputs):
    import concourse.bacc as bacc
    from concourse.bass_utils import run_bass_kernel_spmd

    nc = bacc.Bacc("TRN2", target_bir_lowering=False, num_devices=1)
    arrays, aps = {}, {}
    data = {**layouts(**{k: np.asarray(v) for k, v in inputs.items()}), **constants()}
    for name, v in data.items():
        v = np.ascontiguousarray(v)
        arrays[f"{name}_dram"] = v
        aps[name] = nc.dram_tensor(f"{name}_dram", v.shape, mybir.dt.from_np(v.dtype), kind="ExternalInput").ap()
    out = nc.dram_tensor("out_dram", (T, DIM), mybir.dt.float32, kind="ExternalOutput").ap()
    build(nc, aps, out)
    r = run_bass_kernel_spmd(nc, [arrays], core_ids=[0])
    return r.results[0]["out_dram"].reshape(BATCH, TOK, DIM)
```
